# Optimizing a Trainium2 kernel written in Bass

```python
import numpy as np
import jax
import jax.numpy as jnp

def _softmax(x, axis=-1):
    return jax.nn.softmax(x, axis=axis)

def _gelu(x):
    return jax.nn.gelu(x, approximate=True)

def _silu(x):
    return jax.nn.silu(x)

def _sigmoid(x):
    return jax.nn.sigmoid(x)

def _layernorm(x, axis=-1, eps=1e-05):
    m = jnp.mean(x, axis=axis, keepdims=True)
    v = jnp.var(x, axis=axis, keepdims=True)
    return (x - m) / jnp.sqrt(v + eps)

def _scatter_add(tgt, idx, src, axis=0):
    return tgt.at[idx].add(src)

def _segment_sum(src, seg, n):
    return jax.ops.segment_sum(src, seg, n)
kernel_name = 'mk_adaln_d1_jaxref_r4_21b4d1'

def setup_inputs(seed: int=0):
    np.random.seed(seed)
    _w = jnp.asarray

    def _L0_attn_setup():
        import jax, jax.numpy as jnp
        import numpy as np
        B, N, E, H = (1, 1024, 512, 16)
        D = E // H
        DEGREE = 4
        LN_EPS = 1e-05
        ROPE_BASE = 10000.0

        def rope_cos_sin(n, d):
            inv_freq = 1.0 / ROPE_BASE ** (jnp.arange(0, d, 2, dtype=jnp.float32) / d)
            t = jnp.arange(n, dtype=jnp.float32)[:, None] * inv_freq[None, :]
            return (jnp.cos(t), jnp.sin(t))

        def apply_rope(x, cos, sin):
            x1, x2 = jnp.split(x, 2, axis=-1)
            c = cos[None, :, None, :]
            s = sin[None, :, None, :]
            return jnp.concatenate([x1 * c - x2 * s, x1 * s + x2 * c], axis=-1)

        def layernorm(x, scale, bias, eps=LN_EPS):
            m = jnp.mean(x, axis=-1, keepdims=True)
            v = jnp.var(x, axis=-1, keepdims=True)
            return (x - m) * jax.lax.rsqrt(v + eps) * scale + bias

        def polynomial_attention(q, k, v, degree, is_causal):
            a = jnp.einsum('bhnd,bhmd->bhnm', q, k) ** degree
            if is_causal:
                a = jnp.tril(a)
            denom = jnp.sum(a, axis=-1, keepdims=True)
            return jnp.einsum('bhnm,bhmd->bhnd', a / denom, v)
        key = jax.random.key(seed)
        k0, k1, k2 = jax.random.split(key, 3)
        x = jax.random.normal(k0, (B, N, E), dtype=jnp.float32)
        w_qkv = jax.random.normal(k1, (E, 3 * E), dtype=jnp.float32) * (1.0 / np.sqrt(E))
        w_out = jax.random.normal(k2, (E, E), dtype=jnp.float32) * (1.0 / np.sqrt(E))
        ln_scale = jnp.ones((D,), dtype=jnp.float32)
        ln_bias = jnp.zeros((D,), dtype=jnp.float32)
        return {'x': x, 'w_qkv': w_qkv, 'w_out': w_out, 'ln_scale': ln_scale, 'ln_bias': ln_bias}
    _L0_attn_in = _L0_attn_setup()

    def _L0_ffn_setup():
        import jax, jax.numpy as jnp
        import numpy as np

        def _sparsify_2to4(h):
            B, S, I = h.shape
            g = h.reshape(B, S, I // 4, 4)
            a = jnp.abs(g)
            _, idx = jax.lax.top_k(a, 2)
            pos = jnp.arange(4)
            mask = (pos == idx[..., 0:1]) | (pos == idx[..., 1:2])
            return (g * mask.astype(g.dtype)).reshape(B, S, I)
        key = jax.random.key(seed)
        k1, k2, k3, k4 = jax.random.split(key, 4)
        B, S, H, I = (4, 512, 512, 2048)
        x = jax.random.normal(k1, (B, S, H), dtype=jnp.float32)
        w_gate = jax.random.normal(k2, (H, I), dtype=jnp.float32) / np.sqrt(H)
        w_up = jax.random.normal(k3, (H, I), dtype=jnp.float32) / np.sqrt(H)
        w_down = jax.random.normal(k4, (I, H), dtype=jnp.float32) / np.sqrt(I)
        return {'x': x, 'w_gate': w_gate, 'w_up': w_up, 'w_down': w_down}
    _L0_ffn_in = _L0_ffn_setup()
    _L0_c = _w((lambda *s: np.random.randn(*s).astype(np.float32) * 0.05)(1, 512))
    _L0_wmod = _w((lambda *s: np.random.randn(*s).astype(np.float32) * 0.05)(512, 6 * 512) * 512 ** (-0.5))
    _d = {'L0_attn_x': _L0_attn_in['x'], 'L0_attn_w_qkv': _L0_attn_in['w_qkv'], 'L0_attn_w_out': _L0_attn_in['w_out'], 'L0_attn_ln_scale': _L0_attn_in['ln_scale'], 'L0_attn_ln_bias': _L0_attn_in['ln_bias'], 'L0_ffn_w_gate': _L0_ffn_in['w_gate'], 'L0_ffn_w_up': _L0_ffn_in['w_up'], 'L0_ffn_w_down': _L0_ffn_in['w_down'], 'L0_c': _L0_c, 'L0_wmod': _L0_wmod}
    _x0 = _d['L0_attn_x']
    _d['L0_attn_x'] = jax.random.normal(jax.random.fold_in(jax.random.key(seed), 1), (1, 4096, 512), dtype=_x0.dtype)
    del _x0
    return _d

def reference(L0_attn_x, L0_attn_w_qkv, L0_attn_w_out, L0_attn_ln_scale, L0_attn_ln_bias, L0_ffn_w_gate, L0_ffn_w_up, L0_ffn_w_down, L0_c, L0_wmod):

    def _L0_attn_ref(x, w_qkv, w_out, ln_scale, ln_bias):
        import jax, jax.numpy as jnp
        import numpy as np
        B, N, E, H = (1, 1024, 512, 16)
        D = E // H
        DEGREE = 4
        LN_EPS = 1e-05
        ROPE_BASE = 10000.0

        def rope_cos_sin(n, d):
            inv_freq = 1.0 / ROPE_BASE ** (jnp.arange(0, d, 2, dtype=jnp.float32) / d)
            t = jnp.arange(n, dtype=jnp.float32)[:, None] * inv_freq[None, :]
            return (jnp.cos(t), jnp.sin(t))

        def apply_rope(x, cos, sin):
            x1, x2 = jnp.split(x, 2, axis=-1)
            c = cos[None, :, None, :]
            s = sin[None, :, None, :]
            return jnp.concatenate([x1 * c - x2 * s, x1 * s + x2 * c], axis=-1)

        def layernorm(x, scale, bias, eps=LN_EPS):
            m = jnp.mean(x, axis=-1, keepdims=True)
            v = jnp.var(x, axis=-1, keepdims=True)
            return (x - m) * jax.lax.rsqrt(v + eps) * scale + bias

        def polynomial_attention(q, k, v, degree, is_causal):
            a = jnp.einsum('bhnd,bhmd->bhnm', q, k) ** degree
            if is_causal:
                a = jnp.tril(a)
            denom = jnp.sum(a, axis=-1, keepdims=True)
            return jnp.einsum('bhnm,bhmd->bhnd', a / denom, v)
        b, n, e = x.shape
        proj = x @ w_qkv
        q, k, v = jnp.split(proj, 3, axis=-1)
        q = q.reshape(b, n, H, D)
        k = k.reshape(b, n, H, D)
        v = v.reshape(b, n, H, D)
        cos, sin = rope_cos_sin(n, D)
        q = apply_rope(q, cos, sin)
        k = apply_rope(k, cos, sin)
        q = q.transpose(0, 2, 1, 3)
        k = k.transpose(0, 2, 1, 3)
        v = v.transpose(0, 2, 1, 3)
        q = layernorm(q, ln_scale, ln_bias)
        k = layernorm(k, ln_scale, ln_bias)
        out = polynomial_attention(q, k, v, DEGREE, True)
        out = out.transpose(0, 2, 1, 3).reshape(b, n, e)
        out = out @ w_out
        return out

    def _L0_ffn_ref(x, w_gate, w_up, w_down):
        import jax, jax.numpy as jnp
        import numpy as np

        def _sparsify_2to4(h):
            B, S, I = h.shape
            g = h.reshape(B, S, I // 4, 4)
            a = jnp.abs(g)
            _, idx = jax.lax.top_k(a, 2)
            pos = jnp.arange(4)
            mask = (pos == idx[..., 0:1]) | (pos == idx[..., 1:2])
            return (g * mask.astype(g.dtype)).reshape(B, S, I)
        h = jax.nn.silu(jnp.einsum('bsh,hi->bsi', x, w_gate)) * jnp.einsum('bsh,hi->bsi', x, w_up)
        h_sparse = _sparsify_2to4(h)
        return jnp.einsum('bsi,ih->bsh', h_sparse, w_down)
    x = L0_attn_x
    mod = (_silu(L0_c) @ L0_wmod).reshape(L0_c.shape[0], 6, 1, -1)
    sa, ca, ga, sb, cb, gb = (mod[:, 0], mod[:, 1], mod[:, 2], mod[:, 3], mod[:, 4], mod[:, 5])
    ga = (2 * (ga >= 0) - 1) * jnp.maximum(jnp.abs(ga), 0.25)
    gb = (2 * (gb >= 0) - 1) * jnp.maximum(jnp.abs(gb), 0.25)
    h = _layernorm(x, axis=-1) * (1 + ca) + sa
    x = x + ga * _L0_attn_ref(h, L0_attn_w_qkv, L0_attn_w_out, L0_attn_ln_scale, L0_attn_ln_bias)
    h = _layernorm(x, axis=-1) * (1 + cb) + sb
    x = x + gb * _L0_ffn_ref(h, L0_ffn_w_gate, L0_ffn_w_up, L0_ffn_w_down)
    return x

_drawn_inputs = setup_inputs


def setup_inputs(seed=0):
    import zlib

    import numpy as np

    out = dict(_drawn_inputs(seed))
    spreads = {'L0_attn_ln_scale': (1.0, 0.6), 'L0_attn_ln_bias': (0.0, 2.0)}
    factors = {'L0_attn_w_qkv': 3.977, 'L0_attn_w_out': 3.865}
    for name, (base, spread) in spreads.items():
        noise = np.random.default_rng([zlib.crc32(name.encode()), seed]).standard_normal(out[name].shape)
        drawn = base * np.exp(spread * noise) if base else spread * noise
        out[name] = jnp.asarray(drawn.astype(out[name].dtype))
    for name, factor in factors.items():
        out[name] = (out[name] * factor).astype(out[name].dtype)
    return out
```

```python
from contextlib import ExitStack

import numpy as np

import concourse.bass as bass
from concourse import mybir

F32 = mybir.dt.float32
F32R = mybir.dt.float32r
BF16 = mybir.dt.bfloat16
ALU = mybir.AluOpType
ACT = mybir.ActivationFunctionType
AX = mybir.AxisListType

P = 128
N = 4096
E = 512
H = 16
D = E // H
INNER = 2048
KT = E // P
NB = N // P
CHUNK = 512
NCH = N // CHUNK
BPC = CHUNK // P
HPG = P // D
NG = H // HPG
EPS = 1e-5
START = 1
ROPE_BASE = 10000.0


def setup_phase(nc, keep, ins):
    with ExitStack() as ctx:
        sb = lambda name, shape, dt=F32: ctx.enter_context(nc.sbuf_tensor(name, shape, dt))
        sem = lambda name: ctx.enter_context(nc.semaphore(name))
        ident, gate_a, gate_b, cols = keep["ident"], keep["gate_a"], keep["gate_b"], keep["cols"]

        c_col = sb("c_col", [P, KT])
        silu_c = sb("silu_c", [P, KT])
        silu_wide = sb("silu_wide", [P, KT, P])
        wmod = sb("wmod", [P, KT, 6 * E])
        mod = sb("mod", [P, 6, E])
        gate_abs = sb("gate_abs", [P, 2, E])
        gate_neg = sb("gate_neg", [P, 2, E])
        gate_sign = sb("gate_sign", [P, 2, E])
        picked = sb("picked", [P, 4 * KT, P])
        mod_ps = [ctx.enter_context(nc.psum_tensor(f"mod_ps{s}", [P, E], F32)) for s in range(6)]

        c_loaded = sem("c_loaded")
        wmod_loaded = [sem(f"wmod_loaded{s}") for s in range(6)]
        ident_zero = sem("ident_zero")
        ident_ready = sem("ident_ready")
        silu_done = sem("silu_done")
        wide_done = sem("wide_done")
        mod_summed = sem("mod_summed")
        mod_copied = sem("mod_copied")
        gate_step = sem("gate_step")
        cols_loaded = sem("cols_loaded")

        wmod_v = ins["wmod"].rearrange("(k p) n -> p k n", p=P)
        block = ctx.enter_context(nc.Block())

        @block.sync
        def _(sp):
            sp.dma_start(c_col[:, :], ins["c"].rearrange("o (k p) -> p (o k)", p=P), allow_slow_non_contiguous=True).then_inc(c_loaded, 16)
            for s in range(6):
                sp.dma_start(wmod[:, :, s * E:(s + 1) * E], wmod_v[:, :, s * E:(s + 1) * E]).then_inc(wmod_loaded[s], 16)
            for h in range(HPG):
                sp.dma_start(keep["qk_scale"][h * D:(h + 1) * D, :], ins["ln_scale"].unsqueeze(1)).then_inc(cols_loaded, 16)
                sp.dma_start(keep["qk_bias"][h * D:(h + 1) * D, :], ins["ln_bias"].unsqueeze(1)).then_inc(cols_loaded, 16)
            sp.wait_ge(cols_loaded, 2 * HPG * 16)

        @block.gpsimd
        def _(pool):
            pool.memset(ident[:, :], 0.0).then_inc(ident_zero, 1)
            pool.wait_ge(ident_zero, 1)
            pool.affine_select(out=ident[:, :], in_=ident[:, :], compare_op=ALU.not_equal, fill=1.0,
                               base=0, pattern=[[-1, P]], channel_multiplier=1).then_inc(ident_ready, 1)

        @block.scalar
        def _(act):
            act.wait_ge(c_loaded, 16)
            act.activation(silu_c[:, :], c_col[:, :], ACT.Silu).then_inc(silu_done, 1)
            act.wait_ge(silu_done, 1)
            for k in range(KT):
                wide = act.activation(silu_wide[:, k, :], silu_c[:, k:k + 1].broadcast_to([P, P]), ACT.Copy)
            wide.then_inc(wide_done, 1)
            for s in range(6):
                act.wait_ge(mod_summed, s + 1)
                act.activation(mod[:, s, :], mod_ps[s][:, :], ACT.Copy).then_inc(mod_copied, 1)

        @block.tensor
        def _(pe):
            pe.wait_ge(wide_done, 1)
            for s in range(6):
                pe.wait_ge(wmod_loaded[s], 16)
                for k in range(KT):
                    mm = pe.matmul(mod_ps[s][:, :], silu_wide[:, k, :], wmod[:, k, s * E:(s + 1) * E],
                                   start=(k == 0), stop=(k == KT - 1))
                mm.then_inc(mod_summed, 1)

        @block.vector
        def _(dve):
            dve.memset(keep["eps"][:, :], EPS)
            dve.wait_ge(ident_ready, 1)
            for n, s in enumerate((0, 1, 3, 4)):
                dve.wait_ge(mod_copied, s + 1)
                for k in range(KT):
                    dve.scalar_tensor_tensor(
                        out=picked[:, n * KT + k, :], in0=mod[:, s, k * P:(k + 1) * P], scalar=1.0 if s in (1, 4) else 0.0,
                        in1=ident[:, :], op0=ALU.add, op1=ALU.mult, accum_out=cols[:, n, k:k + 1])
            steps = 0
            for n, (s, gate) in enumerate(((2, gate_a), (5, gate_b))):
                dve.wait_ge(mod_copied, s + 1)
                dve.scalar_tensor_tensor(out=gate_neg[:, n, :], in0=mod[:, s, :], scalar=-1.0, in1=mod[:, s, :],
                                         op0=ALU.mult, op1=ALU.max).then_inc(gate_step, 1)
                dve.tensor_scalar(gate_sign[:, n, :], mod[:, s, :], 0.0, 2.0, ALU.is_ge, ALU.mult).then_inc(gate_step, 1)
                dve.wait_ge(gate_step, steps + 2)
                dve.tensor_scalar(gate_abs[:, n, :], gate_neg[:, n, :], 0.25, None, ALU.max).then_inc(gate_step, 1)
                dve.wait_ge(gate_step, steps + 3)
                dve.scalar_tensor_tensor(out=gate[:, :], in0=gate_sign[:, n, :], scalar=-1.0, in1=gate_abs[:, n, :],
                                         op0=ALU.add, op1=ALU.mult).then_inc(gate_step, 1)
                steps += 4


def projection_phase(nc, keep, ins, qk_scr, v_scr):
    with ExitStack() as ctx:
        sb = lambda name, shape, dt=F32: ctx.enter_context(nc.sbuf_tensor(name, shape, dt))
        pb = lambda name, shape: ctx.enter_context(nc.psum_tensor(name, shape, F32))
        sem = lambda name: ctx.enter_context(nc.semaphore(name))
        ident, cols, eps = keep["ident"], keep["cols"], keep["eps"]
        QK = 2 * E
        QKH = 2 * H
        HALF = D // 2

        wqkv = sb("wqkv", [P, KT, 3 * E])
        x_in = [sb(f"x_in{i}", [P, E]) for i in range(2)]
        rope = [sb(f"rope{i}", [P, 2, D]) for i in range(2)]
        x_stats = sb("x_stats", [P, 6])
        x_mv = sb("x_mv", [P, 2])
        x_std = sb("x_std", [P, 1])
        x_rstd = sb("x_rstd", [P, 1])
        xn = [sb(f"xn{i}", [P, E]) for i in range(2)]
        hT = [sb(f"hT{i}", [P, KT, P]) for i in range(2)]
        rot_cos = sb("rot_cos", [P, QKH, D])
        rot_sin = sb("rot_sin", [P, QKH, D])
        rot = sb("rot", [P, QKH, D])
        hsum = sb("hsum", [P, QKH])
        hmean = sb("hmean", [P, QKH])
        cent = [sb(f"cent{i}", [P, QKH, D]) for i in range(2)]
        csq = sb("csq", [P, QKH, D])
        hvar = sb("hvar", [P, QKH])
        hstd = sb("hstd", [P, QKH])
        hrstd = sb("hrstd", [P, QKH])
        qkn = sb("qkn", [P, QKH, D])
        qkT = sb("qkT", [P, QK])
        qk_round = [sb(f"qk_round{i}", [P, QK // P, P], F32R) for i in range(2)]
        qk_rest = [sb(f"qk_rest{i}", [P, QK // P, P], F32R) for i in range(2)]
        v_out = [sb(f"v_out{i}", [P, E]) for i in range(2)]

        xT_ps = pb("xT_ps", [P, KT, P])
        qk_ps = [pb(f"qk_ps{i}", [P, QKH, D]) for i in range(2)]
        v_ps = pb("v_ps", [P, E])
        qkT_ps = pb("qkT_ps", [P, QK])

        wqkv_loaded = sem("wqkv_loaded")
        x_loaded = [sem(f"x_loaded{i}") for i in range(2)]
        rope_loaded = [sem(f"rope_loaded{i}") for i in range(2)]
        xstat_done = sem("xstat_done")
        aggregate_open = sem("aggregate_open")
        xstd_done = sem("xstd_done")
        xrstd_done = sem("xrstd_done")
        xn_ready = sem("xn_ready")
        xT_ready = sem("xT_ready")
        hT_ready = sem("hT_ready")
        qk_summed = sem("qk_summed")
        v_summed = sem("v_summed")
        v_ready = sem("v_ready")
        parts_ready = sem("parts_ready")
        rot_ready = sem("rot_ready")
        hsum_done = sem("hsum_done")
        hmean_ready = sem("hmean_ready")
        cent_ready = sem("cent_ready")
        csq_ready = sem("csq_ready")
        hvar_ready = sem("hvar_ready")
        hstd_ready = sem("hstd_ready")
        hrstd_ready = sem("hrstd_ready")
        qkn_ready = sem("qkn_ready")
        turned = sem("turned")
        qkT_ready = sem("qkT_ready")
        round_ready = sem("round_ready")
        rest_ready = sem("rest_ready")
        round_stored = [sem(f"round_stored{i}") for i in range(2)]
        rest_stored = [sem(f"rest_stored{i}") for i in range(2)]
        v_stored = [sem(f"v_stored{i}") for i in range(2)]

        x_v = ins["x"].rearrange("o (t p) e -> (o t) p e", p=P)
        rope_v = ins["rope"].rearrange("(t p) a d -> t p a d", p=P)
        v_dst = v_scr.rearrange("(t p) e -> t p e", p=P)
        qk_dst = qk_scr.rearrange("a (c p) n -> a p c n", p=P)

        FIRST, PEELED, LAST = -2, 6, NB + 2

        def live(t):
            return not isinstance(t, int) or 0 <= t < NB

        def steps(eng, step):
            for s in range(FIRST, PEELED):
                step(s, s % 2)
            with eng.Fori(0, (NB - 2 - PEELED) // 2) as i:
                for b in range(2):
                    step(i * 2 + (PEELED + b), b)
            for s in range(NB - 2, LAST + 1):
                step(s, s % 2)

        def wait(eng, s, value):
            if not isinstance(value, int) or value > 0:
                eng.wait_ge(s, value)

        def dmas(t, par):
            return (t - par) * 8

        block = ctx.enter_context(nc.Block())

        @block.sync
        def _(sp):
            def step(s, par):
                if live(s + 2):
                    t = s + 2
                    wait(sp, xn_ready, t - 1)
                    sp.dma_start(x_in[par][:, :], x_v[t]).then_inc(x_loaded[par], 16)
                if isinstance(s, int) and s == -1:
                    for k in range(KT):
                        sp.dma_start(wqkv[:, k, :], ins["w_qkv"][k * P:(k + 1) * P, :]).then_inc(wqkv_loaded, 16)
                if live(s):
                    wait(sp, parts_ready, s - 1)
                    sp.dma_start(rope[par][:, :, :], rope_v[s]).then_inc(rope_loaded[par], 16)
                if live(s - 1):
                    wait(sp, v_ready, s)
                    sp.dma_start(v_dst[s - 1], v_out[1 - par][:, :]).then_inc(v_stored[1 - par], 16)
                if live(s - 3):
                    t, odd = s - 3, 1 - par
                    wait(sp, round_ready, t + 1)
                    sp.dma_start(qk_dst[0, :, :, bass.ts(t, P)], qk_round[odd][:, :, :].bitcast(F32)).then_inc(round_stored[odd], 16)
                    wait(sp, rest_ready, t + 1)
                    sp.dma_start(qk_dst[1, :, :, bass.ts(t, P)], qk_rest[odd][:, :, :].bitcast(F32)).then_inc(rest_stored[odd], 16)

            steps(sp, step)
            for par in range(2):
                sp.wait_ge(v_stored[par], NB // 2 * 16)
                sp.wait_ge(round_stored[par], NB // 2 * 16)
                sp.wait_ge(rest_stored[par], NB // 2 * 16)

        @block.tensor
        def _(pe):
            def step(s, par):
                if live(s + 1):
                    t = s + 1
                    wait(pe, xn_ready, t + 1)
                    wait(pe, hT_ready, t)
                    for k in range(KT):
                        mm = pe.transpose(xT_ps[:, k, :], xn[1 - par][:, k * P:(k + 1) * P], ident[:, :])
                    mm.then_inc(xT_ready, 1)
                if live(s - 3):
                    t = s - 3
                    wait(pe, qkn_ready, t + 1)
                    wait(pe, qkT_ready, t)
                    for c in range(QK // P):
                        mm = pe.transpose(qkT_ps[:, c * P:(c + 1) * P], qkn[:, c * HPG:(c + 1) * HPG, :], ident[:, :])
                    mm.then_inc(turned, 1)
                if live(s):
                    wait(pe, hT_ready, s + 1)
                    wait(pe, parts_ready, s - 1)
                    if isinstance(s, int) and s == 0:
                        pe.wait_ge(wqkv_loaded, KT * 16)
                    for c in range(2):
                        for k in range(KT):
                            mm = pe.matmul(qk_ps[par][:, c * H:(c + 1) * H, :], hT[par][:, k, :],
                                           wqkv[:, k, c * E:(c + 1) * E], start=(k == 0), stop=(k == KT - 1))
                    mm.then_inc(qk_summed, 1)
                    wait(pe, v_ready, s)
                    for k in range(KT):
                        mm = pe.matmul(v_ps[:, :], hT[par][:, k, :], wqkv[:, k, 2 * E:3 * E],
                                       start=(k == 0), stop=(k == KT - 1))
                    mm.then_inc(v_summed, 1)

            steps(pe, step)

        @block.vector
        def _(dve):
            def step(s, par):
                odd = 1 - par
                if live(s + 1):
                    t = s + 1
                    wait(dve, xT_ready, t + 1)
                    wait(dve, v_summed, t - 1)
                    for k in range(KT):
                        op = dve.tensor_scalar(hT[odd][:, k, :], xT_ps[:, k, :], cols[:, 1, k:k + 1],
                                               cols[:, 0, k:k + 1], ALU.mult, ALU.add)
                    op.then_inc(hT_ready, 1)
                if live(s - 1):
                    t = s - 1
                    wait(dve, qk_summed, t + 1)
                    wait(dve, rope_loaded[odd], dmas(t, odd) + 16)
                    wait(dve, rot_ready, t)
                    table = rope[odd]
                    dve.tensor_tensor(rot_cos[:, :, :], qk_ps[odd][:, :, :],
                                      table[:, 0:1, :].broadcast_to([P, QKH, D]), ALU.mult)
                    dve.tensor_tensor(rot_sin[:, :, 0:HALF], qk_ps[odd][:, :, HALF:D],
                                      table[:, 1:2, 0:HALF].broadcast_to([P, QKH, HALF]), ALU.mult)
                    dve.tensor_tensor(rot_sin[:, :, HALF:D], qk_ps[odd][:, :, 0:HALF],
                                      table[:, 1:2, HALF:D].broadcast_to([P, QKH, HALF]), ALU.mult).then_inc(parts_ready, 1)
                if live(s - 2):
                    t = s - 2
                    wait(dve, csq_ready, t + 1)
                    dve.tensor_reduce(hvar[:, :], csq[:, :, :], AX.X, ALU.add).then_inc(hvar_ready, 1)
                if live(s + 2):
                    t = s + 2
                    wait(dve, x_loaded[par], dmas(t, par) + 16)
                    wait(dve, xrstd_done, t)
                    dve.bn_stats(x_stats[:, :], x_in[par][:, :]).then_inc(xstat_done, 1)
                    wait(dve, xstat_done, t * 2 + 1)
                if live(s - 3):
                    t = s - 3
                    wait(dve, qkT_ready, t + 1)
                    wait(dve, round_stored[odd], dmas(t, odd))
                    dve.tensor_copy(qk_round[odd][:, :, :].rearrange("p c n -> p (c n)"), qkT[:, :]).then_inc(round_ready, 1)
                if live(s + 2):
                    wait(dve, xn_ready, s + 2)
                    dve.sem_inc(aggregate_open, 1)
                    dve.bn_aggr(x_mv[:, :], x_stats[:, :]).then_inc(xstat_done, 1)
                if live(s - 2):
                    t = s - 2
                    wait(dve, hstd_ready, t + 1)
                    dve.reciprocal(hrstd[:, :], hstd[:, :]).then_inc(hrstd_ready, 1)
                if live(s + 2):
                    t = s + 2
                    wait(dve, xstd_done, t + 1)
                    dve.reciprocal(x_rstd[:, :], x_std[:, :]).then_inc(xrstd_done, 1)
                if live(s - 2):
                    t = s - 2
                    wait(dve, hrstd_ready, t + 1)
                    wait(dve, turned, t)
                    dve.tensor_tensor(qkn[:, :, :], cent[par][:, :, :],
                                      hrstd[:, :].unsqueeze(2).broadcast_to([P, QKH, D]), ALU.mult).then_inc(qkn_ready, 1)
                if live(s + 2):
                    t = s + 2
                    wait(dve, xrstd_done, t + 1)
                    wait(dve, xT_ready, t - 1)
                    dve.tensor_scalar(xn[par][:, :], x_in[par][:, :], x_mv[:, 0:1], x_rstd[:, :],
                                      ALU.subtract, ALU.mult).then_inc(xn_ready, 1)
                if live(s - 1):
                    t = s - 1
                    wait(dve, rot_ready, t + 1)
                    dve.tensor_reduce(hsum[:, :], rot[:, :, :], AX.X, ALU.add).then_inc(hsum_done, 1)
                    wait(dve, hsum_done, t + 1)
                    wait(dve, cent_ready, t)
                    dve.tensor_scalar(hmean[:, :], hsum[:, :], 1.0 / D, None, ALU.mult).then_inc(hmean_ready, 1)

            steps(dve, step)

        @block.scalar
        def _(act):
            def step(s, par):
                odd = 1 - par
                if live(s - 2):
                    t = s - 2
                    wait(act, cent_ready, t + 1)
                    wait(act, hvar_ready, t)
                    act.activation(csq[:, :, :], cent[par][:, :, :], ACT.Square).then_inc(csq_ready, 1)
                if live(s - 3):
                    t = s - 3
                    wait(act, turned, t + 1)
                    wait(act, round_ready, t)
                    wait(act, rest_ready, t)
                    act.activation(qkT[:, :], qkT_ps[:, :], ACT.Identity, bias=keep["qk_bias"][:, :],
                                   scale=keep["qk_scale"][:, :]).then_inc(qkT_ready, 1)
                if live(s - 1):
                    t = s - 1
                    wait(act, v_summed, t + 1)
                    wait(act, v_stored[odd], dmas(t, odd))
                    act.activation(v_out[odd][:, :], v_ps[:, :], ACT.Copy).then_inc(v_ready, 1)
                if live(s - 2):
                    t = s - 2
                    wait(act, hvar_ready, t + 1)
                    act.activation(hstd[:, :], hvar[:, :], ACT.Sqrt, bias=eps[:, :], scale=1.0 / D).then_inc(hstd_ready, 1)
                if live(s + 2):
                    t = s + 2
                    wait(act, xstat_done, t * 2 + 2)
                    act.activation(x_std[:, :], x_mv[:, 1:2], ACT.Sqrt, bias=eps[:, :]).then_inc(xstd_done, 1)

            steps(act, step)

        @block.gpsimd
        def _(pool):
            def step(s, par):
                odd = 1 - par
                if live(s - 1):
                    t = s - 1
                    wait(pool, parts_ready, t + 1)
                    wait(pool, hsum_done, t)
                    wait(pool, cent_ready, t)
                    pool.tensor_tensor(rot[:, :, :], rot_cos[:, :, :], rot_sin[:, :, :], ALU.add).then_inc(rot_ready, 1)
                if live(s - 3):
                    t = s - 3
                    wait(pool, round_ready, t + 1)
                    wait(pool, rest_stored[odd], dmas(t, odd))
                    pool.tensor_tensor(qk_rest[odd][:, :, :].rearrange("p c n -> p (c n)"), qkT[:, :],
                                       qk_round[odd][:, :, :].rearrange("p c n -> p (c n)").bitcast(F32),
                                       ALU.subtract).then_inc(rest_ready, 1)
                if live(s - 1):
                    t = s - 1
                    wait(pool, hmean_ready, t + 1)
                    wait(pool, qkn_ready, t - 1)
                    wait(pool, csq_ready, t - 1)
                    pool.tensor_tensor(cent[odd][:, :, :], rot[:, :, :],
                                       hmean[:, :].unsqueeze(2).broadcast_to([P, QKH, D]), ALU.subtract).then_inc(cent_ready, 1)

            steps(pool, step)


def attention_phase(nc, keep, qk_scr, v_scr, att_scr):
    with ExitStack() as ctx:
        sb = lambda name, shape, dt=F32: ctx.enter_context(nc.sbuf_tensor(name, shape, dt))
        sem = lambda name: ctx.enter_context(nc.semaphore(name))
        QBUF, SQBUF, POWBUF, LAG = 4, 3, 5, 3
        PAIR = 2
        HALVES = HPG // PAIR

        k_stack = sb("k_stack", [P, HPG, N], F32R)
        v_grp = sb("v_grp", [P, NB, P])
        q_stack = [sb(f"q_stack{i}", [P, HPG, CHUNK], F32R) for i in range(QBUF)]
        squares = [sb(f"squares{i}", [P, PAIR, CHUNK]) for i in range(SQBUF)]
        powers = [sb(f"powers{i}", [P, PAIR, CHUNK]) for i in range(POWBUF)]
        ones = sb("ones", [P, D])
        inv_den = sb("inv_den", [P, CHUNK])
        att = [sb(f"att{i}", [P, CHUNK]) for i in range(2)]
        score_ps = [ctx.enter_context(nc.psum_tensor(f"score_ps{i}", [P, PAIR, CHUNK], F32)) for i in range(2)]
        num_ps = [ctx.enter_context(nc.psum_tensor(f"num_ps{i}", [P, CHUNK], F32)) for i in range(2)]
        den_ps = [ctx.enter_context(nc.psum_tensor(f"den_ps{i}", [P, CHUNK], F32)) for i in range(2)]

        k_loaded = [sem(f"k_loaded{c}") for c in range(NCH)]
        q_loaded = [sem(f"q_loaded{i}") for i in range(QBUF)]
        kv_free = sem("kv_free")
        q_free = sem("q_free")
        ones_ready = sem("ones_ready")
        scores_ready = sem("scores_ready")
        squares_ready = sem("squares_ready")
        masked_ready = sem("masked_ready")
        select_open = sem("select_open")
        powers_ready = sem("powers_ready")
        powers_used = sem("powers_used")
        inverse_ready = sem("inverse_ready")
        att_ready = sem("att_ready")
        att_stored = [sem(f"att_stored{i}") for i in range(2)]

        half_steps = [(j, i, half) for j in range(NCH) for i in range(BPC * (j + 1)) for half in range(HALVES)]
        U = len(half_steps)
        diagonals = [u for u, (j, i, half) in enumerate(half_steps) if i >= BPC * j]
        chunk_end = [max(u for u, x in enumerate(half_steps) if x[0] == j) for j in range(NCH)]
        last_use = {max(u for u, x in enumerate(half_steps) if x[1] == BPC * c + BPC - 1): c for c in range(NCH)}

        def first_query(u):
            j, i, _ = half_steps[u]
            return max(0, i - BPC * j) * P

        k_src = qk_scr[:, E:2 * E, :].rearrange("a (g h d) n -> a g d h n", g=NG, h=HPG)
        q_src = qk_scr[:, 0:E, :].rearrange("a (g h d) n -> a g d h n", g=NG, h=HPG)
        v_src = v_scr.rearrange("(t p) (g e) -> g p t e", p=P, g=NG)
        att_dst = att_scr.rearrange("(g p) n -> g p n", g=NG)
        Q_PARTS = (0, 0, 1, 1)
        K_PARTS = (0, 1, 0, 1)
        KV_DMAS = len(K_PARTS) + 1
        block = ctx.enter_context(nc.Block())

        @block.sync
        def _(sp):
            with sp.Fori(0, NG) as g:
                for c in range(NCH):
                    sp.wait_ge(kv_free, g * NCH + (c + 1))
                    for a, part in enumerate(K_PARTS):
                        sp.dma_start(k_stack[a * D:(a + 1) * D, :, c * CHUNK:(c + 1) * CHUNK].bitcast(F32),
                                     k_src[part, g, :, :, c * CHUNK:(c + 1) * CHUNK]).then_inc(k_loaded[c], 16)
                    sp.dma_start(v_grp[:, c * BPC:(c + 1) * BPC, :],
                                 v_src[g, :, c * BPC:(c + 1) * BPC, :]).then_inc(k_loaded[c], 16)
                    sp.wait_ge(ones_ready, 1)
                    sp.wait_ge(q_free, g * NCH + (c + 1))
                    for a, part in enumerate(Q_PARTS):
                        sp.dma_start(q_stack[c % QBUF][a * D:(a + 1) * D, :, :].bitcast(F32),
                                     q_src[part, g, :, :, c * CHUNK:(c + 1) * CHUNK]).then_inc(q_loaded[c % QBUF], 16)

        @block.tensor
        def _(pe):
            pe.sem_inc(powers_used, START)
            pe.sem_inc(kv_free, NCH)
            pe.sem_inc(q_free, QBUF)
            pe.wait_ge(ones_ready, 1)

            def scores(g, u):
                j, i, half = half_steps[u]
                n0 = first_query(u)
                if i == 0 and half == 0:
                    pe.wait_ge(q_loaded[j % QBUF], (g * (NCH // QBUF) + (j // QBUF + 1)) * (16 * len(Q_PARTS)))
                if i == BPC * j and half == 0:
                    pe.wait_ge(k_loaded[j], (g + 1) * (16 * KV_DMAS))
                pe.wait_ge(squares_ready, g * U + max(u - 1, 0) + START)
                for h in range(PAIR):
                    hh = half * PAIR + h
                    mm = pe.matmul(score_ps[u % 2][:, h, n0:], k_stack[:, hh, i * P:(i + 1) * P],
                                   q_stack[j % QBUF][:, hh, n0:], start=True, stop=True)
                mm.then_inc(scores_ready, 1)

            def weigh(g, st):
                j, i, _ = half_steps[HALVES * st]
                n0 = first_query(HALVES * st)
                first, last = i == 0, i == BPC * (j + 1) - 1
                if first:
                    pe.wait_ge(att_ready, g * NCH + max(j - 1, 0) + START)
                for half in range(HALVES):
                    u = HALVES * st + half
                    pe.wait_ge(powers_ready, g * U + (u + 1) + START)
                    for h in range(PAIR):
                        hh = half * PAIR + h
                        mm = pe.matmul(num_ps[j % 2][hh * D:(hh + 1) * D, n0:], v_grp[:, i, hh * D:(hh + 1) * D],
                                       powers[u % POWBUF][:, h, n0:], start=first, stop=last)
                if HALVES * st + 1 in last_use:
                    mm.then_inc(kv_free, 1)
                for half in range(HALVES):
                    u = HALVES * st + half
                    for h in range(PAIR):
                        hh = half * PAIR + h
                        mm = pe.matmul(den_ps[j % 2][hh * D:(hh + 1) * D, n0:], ones[:, :],
                                       powers[u % POWBUF][:, h, n0:], start=first, stop=last)
                        if h == 0 and u in chunk_end:
                            mm.then_inc(q_free, 1)
                    mm.then_inc(powers_used, 1)

            with pe.Fori(0, NG) as g:
                for st in range(U // HALVES + 1):
                    if st < U // HALVES:
                        for half in range(HALVES):
                            scores(g, HALVES * st + half)
                    if st >= 1:
                        weigh(g, st - 1)

        @block.scalar
        def _(act):
            act.sem_inc(squares_ready, START)
            with act.Fori(0, NG) as g:
                for u in range(U):
                    n0 = first_query(u)
                    act.wait_ge(scores_ready, g * U + (u + 1))
                    act.wait_ge(powers_ready, g * U + max(u - SQBUF + 1, 0) + START)
                    act.activation(squares[u % SQBUF][:, :, n0:], score_ps[u % 2][:, :, n0:], ACT.Square).then_inc(squares_ready, 1)

        @block.gpsimd
        def _(pool):
            with pool.Fori(0, NG) as g:
                for n, u in enumerate(diagonals):
                    n0 = first_query(u)
                    pool.wait_ge(squares_ready, g * U + (u + 1) + START)
                    pool.sem_inc(select_open, 1)
                    corner = squares[u % SQBUF][:, :, n0:n0 + P]
                    pool.affine_select(out=corner, in_=corner, compare_op=ALU.is_ge, fill=0.0, base=0,
                                       pattern=[[0, PAIR], [1, P]], channel_multiplier=-1).then_inc(masked_ready, 1)
                    if u in chunk_end:
                        j = half_steps[u][0]
                        pool.wait_ge(att_ready, g * NCH + (j + 1) + START)
                        pool.dma_start(att_dst[g, :, j * CHUNK:(j + 1) * CHUNK], att[j % 2][:, :]).then_inc(att_stored[j % 2], 16)
            for i in range(2):
                pool.wait_ge(att_stored[i], NG * NCH // 2 * 16)

        @block.vector
        def _(dve):
            dve.sem_inc(powers_ready, START)
            dve.sem_inc(att_ready, START)
            dve.memset(ones[:, :], 1.0).then_inc(ones_ready, 1)

            def normalise(g, j):
                dve.wait_ge(powers_used, g * U + (chunk_end[j] + 1) + START)
                dve.reciprocal(inv_den[:, :], den_ps[j % 2][:, :]).then_inc(inverse_ready, 1)
                dve.wait_ge(inverse_ready, g * NCH + (j + 1))
                if j >= 2:
                    dve.wait_ge(att_stored[j % 2], (g * (NCH // 2) + j // 2) * 16)
                dve.tensor_tensor(att[j % 2][:, :], num_ps[j % 2][:, :], inv_den[:, :], ALU.mult).then_inc(att_ready, 1)

            with dve.Fori(0, NG) as g:
                for u in range(U):
                    j, i, half = half_steps[u]
                    n0 = first_query(u)
                    if u in diagonals:
                        dve.wait_ge(masked_ready, g * len(diagonals) + (diagonals.index(u) + 1))
                    else:
                        dve.wait_ge(squares_ready, g * U + (u + 1) + START)
                    dve.wait_ge(powers_used, g * U + max(u - POWBUF + 1, 0) + START)
                    sq = squares[u % SQBUF][:, :, n0:]
                    dve.tensor_tensor(powers[u % POWBUF][:, :, n0:], sq, sq, ALU.mult).then_inc(powers_ready, 1)
                    if u - LAG - 1 in chunk_end:
                        normalise(g, half_steps[u - LAG - 1][0])
                normalise(g, NCH - 1)
                for i in range(2):
                    dve.wait_ge(att_stored[i], (g + 1) * (NCH // 2 * 16))


def mlp_phase(nc, keep, ins, att_scr, out):
    with ExitStack() as ctx:
        sb = lambda name, shape, dt=F32: ctx.enter_context(nc.sbuf_tensor(name, shape, dt))
        sem = lambda name: ctx.enter_context(nc.semaphore(name))
        ident, cols, eps = keep["ident"], keep["cols"], keep["eps"]
        PL = 4
        IC = INNER // (PL * P)
        KI = INNER // P

        w_out = sb("w_out", [P, KT, E])
        w_gate = sb("w_gate", [P, KT, INNER])
        w_up = sb("w_up", [P, KT, INNER])
        w_down = sb("w_down", [P, KI, E])
        att = sb("att_in", [P, NG, CHUNK])
        x_in = sb("xr_in", [P, BPC, E])
        x_mid = sb("x_mid", [P, BPC, E])
        stats = sb("stats", [P, BPC, 6])
        mv = sb("mv", [P, BPC, 2])
        std = sb("std", [P, BPC])
        rstd = sb("rstd", [P, BPC])
        xn = sb("xn_mid", [P, BPC, E])
        hT = sb("hT_mid", [P, KT, CHUNK])
        silu = [sb(f"silu{i}", [P, CHUNK]) for i in range(2)]
        hid = sb("hid", [P, PL, CHUNK])
        size = sb("size", [P, PL, CHUNK])
        above1 = sb("above1", [P, 3, CHUNK], BF16)
        above2 = sb("above2", [P, 2, CHUNK], BF16)
        above3 = sb("above3", [P, CHUNK], BF16)
        part = sb("part", [P, PL, CHUNK], BF16)
        score = sb("score", [P, PL, CHUNK], BF16)
        kept = [sb(f"kept{i}", [P, PL, CHUNK]) for i in range(2)]
        ring = [ctx.enter_context(nc.psum_tensor(f"ring{i}", [P, E], F32)) for i in range(4)]
        y_ps = [ctx.enter_context(nc.psum_tensor(f"y_ps{i}", [P, E], F32)) for i in range(BPC)]

        w_out_loaded = sem("w_out_loaded")
        w_in_loaded = sem("w_in_loaded")
        w_down_loaded = sem("w_down_loaded")
        w_out_gated = sem("w_out_gated")
        w_down_gated = sem("w_down_gated")
        att_loaded = sem("att_loaded")
        x_loaded = sem("xr_loaded")
        projected = sem("projected")
        mid_ready = sem("mid_ready")
        stat_step = sem("stat_step")
        norm_open = sem("norm_open")
        std_ready = sem("std_ready")
        rstd_ready = sem("rstd_ready")
        xn_ready = sem("xnm_ready")
        xT_ready = sem("xTm_ready")
        hT_ready = sem("hTm_ready")
        pair_ready = sem("pair_ready")
        silu_ready = sem("silu_ready")
        hid_ready = sem("hid_ready")
        size_ready = sem("size_ready")
        above_ready = sem("above_ready")
        part_ready = sem("part_ready")
        score_ready = sem("score_ready")
        kept_ready = sem("kept_ready")
        kept_used = sem("kept_used")
        y_ready = sem("y_ready")
        out_ready = sem("out_ready")
        out_stored = sem("out_stored")

        x_v = ins["x"].rearrange("o (c b p) e -> (o c) p b e", p=P, b=BPC)
        out_v = out.rearrange("o (c b p) e -> (o c) p b e", p=P, b=BPC)
        att_v = att_scr.rearrange("(g p) (c n) -> c p g n", p=P, n=CHUNK)
        down_v = ins["w_down"].rearrange("(i p a) e -> i p a e", p=P, a=PL)
        gate_v = w_gate[:, :, :].rearrange("p k (i c a) -> p k i a c", c=P, a=PL)
        up_v = w_up[:, :, :].rearrange("p k (i c a) -> p k i a c", c=P, a=PL)
        block = ctx.enter_context(nc.Block())

        @block.sync
        def _(sp):
            sp.dma_start(w_out[:, :, :], ins["w_out"].rearrange("(k p) e -> p k e", p=P)).then_inc(w_out_loaded, 16)
            with sp.Fori(0, NCH) as c:
                sp.wait_ge(projected, c * BPC + START)
                sp.dma_start(att[:, :, :], att_v[c]).then_inc(att_loaded, 16)
                sp.wait_ge(mid_ready, c * BPC + START)
                sp.dma_start(x_in[:, :, :], x_v[c]).then_inc(x_loaded, 16)

        @block.gpsimd
        def _(pool):
            for k in range(KT):
                pool.dma_start(w_gate[:, k, :], ins["w_gate"][k * P:(k + 1) * P, :]).then_inc(w_in_loaded, 16)
                pool.dma_start(w_up[:, k, :], ins["w_up"][k * P:(k + 1) * P, :]).then_inc(w_in_loaded, 16)
            for i in range(IC):
                pool.dma_start(w_down[:, i * PL:(i + 1) * PL, :], down_v[i]).then_inc(w_down_loaded, 16)
            with pool.Fori(0, NCH) as c:
                pool.wait_ge(out_ready, c * BPC + BPC + START)
                pool.dma_start(out_v[c], x_mid[:, :, :]).then_inc(out_stored, 16)
            pool.wait_ge(out_stored, NCH * 16)

        @block.tensor
        def _(pe):
            for counted in (projected, kept_used, y_ready):
                pe.sem_inc(counted, START)
            pe.wait_ge(w_out_gated, 1)

            def project(c):
                pe.wait_ge(att_loaded, (c + 1) * 16)
                for b in range(BPC):
                    if b == 0:
                        pe.wait_ge(hid_ready, c * (IC * PL) + START)
                    for k in range(NG):
                        mm = pe.matmul(ring[b][:, :], att[:, k, b * P:(b + 1) * P], w_out[:, k, :],
                                       start=(k == 0), stop=(k == NG - 1))
                    mm.then_inc(projected, 1)

            def turn(c):
                for k in range(KT):
                    pe.wait_ge(xn_ready, c * BPC + BPC)
                    for b in range(BPC):
                        mm = pe.transpose(ring[k][:, b * P:(b + 1) * P], xn[:, b, k * P:(k + 1) * P], ident[:, :])
                    mm.then_inc(xT_ready, 1)

            def gate_up(c, i):
                for a in range(PL):
                    n = i * PL + a
                    pe.wait_ge(hid_ready, c * (IC * PL) + max(n - 1, 0) + START)
                    if n < 2:
                        pe.wait_ge(hT_ready, (c + 1) * KT)
                    for w, bank in ((gate_v, ring[2 * (n % 2)]), (up_v, ring[2 * (n % 2) + 1])):
                        for k in range(KT):
                            mm = pe.matmul(bank[:, :], w[:, k, i, a, :], hT[:, k, :], start=(k == 0), stop=(k == KT - 1))
                    mm.then_inc(pair_ready, 1)

            def down(c, i):
                pe.wait_ge(kept_ready, c * IC + (i + 1) + START)
                if i == 0:
                    pe.wait_ge(out_ready, c * BPC + START)
                for b in range(BPC):
                    for a in range(PL):
                        mm = pe.matmul(y_ps[b][:, :], kept[i % 2][:, a, b * P:(b + 1) * P], w_down[:, i * PL + a, :],
                                       start=(i == 0 and a == 0), stop=(i == IC - 1 and a == PL - 1))
                    if i == IC - 1:
                        mm.then_inc(y_ready, 1)
                    elif b == BPC - 1:
                        mm.then_inc(kept_used, 1)

            with pe.Fori(0, NCH) as c:
                project(c)
                turn(c)
                pe.wait_ge(w_in_loaded, 2 * KT * 16)
                pe.wait_ge(w_down_gated, KI)
                gate_up(c, 0)
                for i in range(1, IC):
                    gate_up(c, i)
                    down(c, i - 1)
                down(c, IC - 1)

        @block.scalar
        def _(act):
            with act.Fori(0, NCH) as c:
                act.wait_ge(stat_step, c * (2 * BPC) + 2 * BPC)
                act.activation(std[:, :], mv[:, :, 1], ACT.Sqrt, bias=eps[:, :]).then_inc(std_ready, 1)
                for i in range(IC):
                    for a in range(PL):
                        n = i * PL + a
                        act.wait_ge(pair_ready, c * (IC * PL) + (n + 1))
                        act.wait_ge(hid_ready, c * (IC * PL) + max(n - 1, 0) + START)
                        act.activation(silu[n % 2][:, :], ring[2 * (n % 2)][:, :], ACT.Silu).then_inc(silu_ready, 1)
                        if n > 0:
                            m = n - 1
                            act.wait_ge(hid_ready, c * (IC * PL) + (m + 1) + START)
                            if m % PL == 0:
                                act.wait_ge(above_ready, (c * IC + m // PL) * 3 + START)
                            act.activation(size[:, m % PL, :], hid[:, m % PL, :], ACT.Abs).then_inc(size_ready, 1)
                m = IC * PL - 1
                act.wait_ge(hid_ready, (c + 1) * (IC * PL) + START)
                act.activation(size[:, m % PL, :], hid[:, m % PL, :], ACT.Abs).then_inc(size_ready, 1)

        @block.vector
        def _(dve):
            for counted in (mid_ready, hid_ready, above_ready, kept_ready, out_ready):
                dve.sem_inc(counted, START)
            dve.wait_ge(w_out_loaded, 16)
            for k in range(KT):
                op = dve.tensor_tensor(w_out[:, k, :], w_out[:, k, :], keep["gate_a"][:, :], ALU.mult)
            op.then_inc(w_out_gated, 1)
            dve.wait_ge(w_down_loaded, IC * 16)
            for k in range(KI):
                dve.tensor_tensor(w_down[:, k, :], w_down[:, k, :], keep["gate_b"][:, :], ALU.mult).then_inc(w_down_gated, 1)

            def norm(c):
                dve.wait_ge(x_loaded, (c + 1) * 16)
                for b in range(BPC):
                    dve.wait_ge(projected, c * BPC + (b + 1) + START)
                    dve.tensor_tensor(x_mid[:, b, :], ring[b][:, :], x_in[:, b, :], ALU.add).then_inc(mid_ready, 1)
                    dve.wait_ge(mid_ready, c * BPC + (b + 1) + START)
                    dve.bn_stats(stats[:, b, :], x_mid[:, b, :]).then_inc(stat_step, 1)
                dve.wait_ge(stat_step, c * (2 * BPC) + BPC)
                dve.sem_inc(norm_open, 1)
                for b in range(BPC):
                    dve.bn_aggr(mv[:, b, :], stats[:, b, :]).then_inc(stat_step, 1)
                dve.wait_ge(std_ready, c + 1)
                dve.reciprocal(rstd[:, :], std[:, :]).then_inc(rstd_ready, 1)
                dve.wait_ge(rstd_ready, c + 1)
                for b in range(BPC):
                    dve.tensor_scalar(xn[:, b, :], x_mid[:, b, :], mv[:, b, 0:1], rstd[:, b:b + 1],
                                      ALU.subtract, ALU.mult).then_inc(xn_ready, 1)
                for k in range(KT):
                    dve.wait_ge(xT_ready, c * KT + (k + 1))
                    dve.tensor_scalar(hT[:, k, :], ring[k][:, :], cols[:, 3, k:k + 1], cols[:, 2, k:k + 1],
                                      ALU.mult, ALU.add).then_inc(hT_ready, 1)

            def hidden(c, i):
                dve.wait_ge(kept_ready, c * IC + i + START)
                for a in range(PL):
                    n = i * PL + a
                    dve.wait_ge(silu_ready, c * (IC * PL) + (n + 1))
                    dve.tensor_tensor(hid[:, a, :], ring[2 * (n % 2) + 1][:, :], silu[n % 2][:, :], ALU.mult).then_inc(hid_ready, 1)

            def sparsify(c, i):
                s = c * IC + i
                dve.wait_ge(size_ready, s * PL + PL)
                dve.tensor_tensor(above1[:, :, :], size[:, 0:3, :], size[:, 1:4, :], ALU.is_ge).then_inc(above_ready, 1)
                dve.tensor_tensor(above2[:, :, :], size[:, 0:2, :], size[:, 2:4, :], ALU.is_ge).then_inc(above_ready, 1)
                dve.tensor_tensor(above3[:, :], size[:, 0, :], size[:, 3, :], ALU.is_ge).then_inc(above_ready, 1)
                dve.wait_ge(above_ready, s * 3 + 3 + START)
                dve.tensor_tensor(part[:, 0, :], above1[:, 0, :], above2[:, 0, :], ALU.add).then_inc(part_ready, 1)
                dve.tensor_tensor(part[:, 1, :], above1[:, 1, :], above2[:, 1, :], ALU.add).then_inc(part_ready, 1)
                dve.tensor_tensor(part[:, 2, :], above1[:, 2, :], above2[:, 0, :], ALU.subtract).then_inc(part_ready, 1)
                dve.tensor_tensor(part[:, 3, :], above1[:, 2, :], above2[:, 1, :], ALU.add).then_inc(part_ready, 1)
                dve.wait_ge(part_ready, s * 4 + 4)
                dve.tensor_tensor(score[:, 0, :], part[:, 0, :], above3[:, :], ALU.add).then_inc(score_ready, 1)
                dve.tensor_tensor(score[:, 1, :], part[:, 1, :], above1[:, 0, :], ALU.subtract).then_inc(score_ready, 1)
                dve.tensor_tensor(score[:, 2, :], part[:, 2, :], above1[:, 1, :], ALU.subtract).then_inc(score_ready, 1)
                dve.tensor_tensor(score[:, 3, :], part[:, 3, :], above3[:, :], ALU.add).then_inc(score_ready, 1)
                dve.wait_ge(score_ready, s * 4 + 4)
                if i >= 2:
                    dve.wait_ge(kept_used, c * (IC - 1) + (i - 1) + START)
                else:
                    dve.wait_ge(y_ready, c * BPC + START)
                for a, (test, bound) in enumerate(((ALU.is_ge, 2.0), (ALU.is_ge, 1.0), (ALU.is_ge, 0.0), (ALU.is_le, 1.0))):
                    op = dve.scalar_tensor_tensor(out=kept[i % 2][:, a, :], in0=score[:, a, :], scalar=bound,
                                                  in1=hid[:, a, :], op0=test, op1=ALU.mult)
                op.then_inc(kept_ready, 1)

            with dve.Fori(0, NCH) as c:
                norm(c)
                for i in range(IC):
                    hidden(c, i)
                    sparsify(c, i)
                for b in range(BPC):
                    dve.wait_ge(y_ready, c * BPC + (b + 1) + START)
                    dve.tensor_tensor(x_mid[:, b, :], x_mid[:, b, :], y_ps[b][:, :], ALU.add).then_inc(out_ready, 1)
                dve.wait_ge(out_stored, (c + 1) * 16)


def adaln_kernel(nc, ins, out):
    qk_scr = nc.dram_tensor("qk_scr", [2, 2 * E, N], F32).ap()
    v_scr = nc.dram_tensor("v_scr", [N, E], F32).ap()
    att_scr = nc.dram_tensor("att_scr", [E, N], F32).ap()
    with ExitStack() as ctx:
        sb = lambda name, shape: ctx.enter_context(nc.sbuf_tensor(name, shape, F32))
        keep = {
            "ident": sb("ident", [P, P]),
            "gate_a": sb("gate_a", [P, E]),
            "gate_b": sb("gate_b", [P, E]),
            "cols": sb("cols", [P, 4, KT]),
            "qk_scale": sb("qk_scale", [P, 1]),
            "qk_bias": sb("qk_bias", [P, 1]),
            "eps": sb("eps", [P, 1]),
        }
        setup_phase(nc, keep, ins)
        projection_phase(nc, keep, ins, qk_scr, v_scr)
        attention_phase(nc, keep, qk_scr, v_scr, att_scr)
        mlp_phase(nc, keep, ins, att_scr, out)


_INS = {
    "x": "L0_attn_x", "w_qkv": "L0_attn_w_qkv", "w_out": "L0_attn_w_out", "ln_scale": "L0_attn_ln_scale",
    "ln_bias": "L0_attn_ln_bias", "w_gate": "L0_ffn_w_gate", "w_up": "L0_ffn_w_up", "w_down": "L0_ffn_w_down",
    "c": "L0_c", "wmod": "L0_wmod",
}


def rope_table():
    inv_freq = np.float32(1.0) / np.power(np.float32(ROPE_BASE), np.arange(0, D, 2, dtype=np.float32) / np.float32(D))
    angle = (np.arange(N, dtype=np.float32)[:, None] * inv_freq[None, :]).astype(np.float64)
    cos, sin = np.cos(angle), np.sin(angle)
    table = np.stack([np.concatenate([cos, cos], 1), np.concatenate([-sin, sin], 1)], 1)
    return table.astype(np.float32)


def kernel(**inputs):
    import concourse.bacc as _bacc
    from concourse.bass_utils import run_bass_kernel_spmd as _run

    nc = _bacc.Bacc("TRN2", target_bir_lowering=False, num_devices=1)
    arrays = {f"in_{short}": np.ascontiguousarray(inputs[name]) for short, name in _INS.items()}
    arrays["in_rope"] = rope_table()
    ins = {name[3:]: nc.dram_tensor(name, a.shape, mybir.dt.from_np(a.dtype), kind="ExternalInput").ap()
           for name, a in arrays.items()}
    out = nc.dram_tensor("out", (1, N, E), F32, kind="ExternalOutput").ap()
    adaln_kernel(nc, ins, out)
    r = _run(nc, [arrays], core_ids=[0])
    return r.results[0]["out"]
```

```python
from contextlib import ExitStack

import numpy as np

import concourse.bass as bass
from concourse import mybir

F32 = mybir.dt.float32
F32R = mybir.dt.float32r
BF16 = mybir.dt.bfloat16
F16 = mybir.dt.float16
I32 = mybir.dt.int32
ALU = mybir.AluOpType
ACT = mybir.ActivationFunctionType
AX = mybir.AxisListType
RMAX = bass.bass_isa.ReduceOp.max

P = 128
N = 4096
E = 512
H = 16
D = E // H
INNER = 2048
KT = E // P
NB = N // P
CHUNK = 512
NCH = N // CHUNK
BPC = CHUNK // P
HPG = P // D
NG = H // HPG
EPS = 1e-5
START = 1
ROPE_BASE = 10000.0


def setup_phase(nc, keep, ins):
    with ExitStack() as ctx:
        sb = lambda name, shape, dt=F32: ctx.enter_context(nc.sbuf_tensor(name, shape, dt))
        sem = lambda name: ctx.enter_context(nc.semaphore(name))
        ident, gate_a, gate_b, cols = keep["ident"], keep["gate_a"], keep["gate_b"], keep["cols"]

        c_col = sb("c_col", [P, KT])
        silu_c = sb("silu_c", [P, KT])
        silu_wide = sb("silu_wide", [P, KT, P])
        wmod = sb("wmod", [P, KT, 6 * E])
        mod = sb("mod", [P, 6, E])
        gate_abs = sb("gate_abs", [P, 2, E])
        gate_neg = sb("gate_neg", [P, 2, E])
        gate_sign = sb("gate_sign", [P, 2, E])
        picked = sb("picked", [P, 4 * KT, P])
        mod_ps = [ctx.enter_context(nc.psum_tensor(f"mod_ps{s}", [P, E], F32)) for s in range(6)]

        c_loaded = sem("c_loaded")
        wmod_loaded = [sem(f"wmod_loaded{s}") for s in range(6)]
        ident_zero = sem("ident_zero")
        ident_ready = sem("ident_ready")
        silu_done = sem("silu_done")
        wide_done = sem("wide_done")
        mod_summed = sem("mod_summed")
        mod_copied = sem("mod_copied")
        gate_step = sem("gate_step")
        cols_loaded = sem("cols_loaded")

        wmod_v = ins["wmod"].rearrange("(k p) n -> p k n", p=P)
        block = ctx.enter_context(nc.Block())

        @block.sync
        def _(sp):
            sp.dma_start(c_col[:, :], ins["c"].rearrange("o (k p) -> p (o k)", p=P), allow_slow_non_contiguous=True).then_inc(c_loaded, 16)
            for s in range(6):
                sp.dma_start(wmod[:, :, s * E:(s + 1) * E], wmod_v[:, :, s * E:(s + 1) * E]).then_inc(wmod_loaded[s], 16)
            for h in range(HPG):
                sp.dma_start(keep["qk_scale"][h * D:(h + 1) * D, :], ins["ln_scale"].unsqueeze(1)).then_inc(cols_loaded, 16)
                sp.dma_start(keep["qk_bias"][h * D:(h + 1) * D, :], ins["ln_bias"].unsqueeze(1)).then_inc(cols_loaded, 16)
            sp.wait_ge(cols_loaded, 2 * HPG * 16)

        @block.gpsimd
        def _(pool):
            pool.memset(ident[:, :], 0.0).then_inc(ident_zero, 1)
            pool.wait_ge(ident_zero, 1)
            pool.affine_select(out=ident[:, :], in_=ident[:, :], compare_op=ALU.not_equal, fill=1.0,
                               base=0, pattern=[[-1, P]], channel_multiplier=1).then_inc(ident_ready, 1)

        @block.scalar
        def _(act):
            act.wait_ge(c_loaded, 16)
            act.activation(silu_c[:, :], c_col[:, :], ACT.Silu).then_inc(silu_done, 1)
            act.wait_ge(silu_done, 1)
            for k in range(KT):
                wide = act.activation(silu_wide[:, k, :], silu_c[:, k:k + 1].broadcast_to([P, P]), ACT.Copy)
            wide.then_inc(wide_done, 1)
            for s in range(6):
                act.wait_ge(mod_summed, s + 1)
                act.activation(mod[:, s, :], mod_ps[s][:, :], ACT.Copy).then_inc(mod_copied, 1)

        @block.tensor
        def _(pe):
            pe.wait_ge(wide_done, 1)
            for s in range(6):
                pe.wait_ge(wmod_loaded[s], 16)
                for k in range(KT):
                    mm = pe.matmul(mod_ps[s][:, :], silu_wide[:, k, :], wmod[:, k, s * E:(s + 1) * E],
                                   start=(k == 0), stop=(k == KT - 1))
                mm.then_inc(mod_summed, 1)

        @block.vector
        def _(dve):
            dve.memset(keep["eps"][:, :], EPS)
            dve.wait_ge(ident_ready, 1)
            for n, s in enumerate((0, 1, 3, 4)):
                dve.wait_ge(mod_copied, s + 1)
                for k in range(KT):
                    dve.scalar_tensor_tensor(
                        out=picked[:, n * KT + k, :], in0=mod[:, s, k * P:(k + 1) * P], scalar=1.0 if s in (1, 4) else 0.0,
                        in1=ident[:, :], op0=ALU.add, op1=ALU.mult, accum_out=cols[:, n, k:k + 1])
            steps = 0
            for n, (s, gate) in enumerate(((2, gate_a), (5, gate_b))):
                dve.wait_ge(mod_copied, s + 1)
                dve.scalar_tensor_tensor(out=gate_neg[:, n, :], in0=mod[:, s, :], scalar=-1.0, in1=mod[:, s, :],
                                         op0=ALU.mult, op1=ALU.max).then_inc(gate_step, 1)
                dve.tensor_scalar(gate_sign[:, n, :], mod[:, s, :], 0.0, 2.0, ALU.is_ge, ALU.mult).then_inc(gate_step, 1)
                dve.wait_ge(gate_step, steps + 2)
                dve.tensor_scalar(gate_abs[:, n, :], gate_neg[:, n, :], 0.25, None, ALU.max).then_inc(gate_step, 1)
                dve.wait_ge(gate_step, steps + 3)
                dve.scalar_tensor_tensor(out=gate[:, :], in0=gate_sign[:, n, :], scalar=-1.0, in1=gate_abs[:, n, :],
                                         op0=ALU.add, op1=ALU.mult).then_inc(gate_step, 1)
                steps += 4


def projection_phase(nc, keep, ins, qk_scr, v_scr):
    with ExitStack() as ctx:
        sb = lambda name, shape, dt=F32: ctx.enter_context(nc.sbuf_tensor(name, shape, dt))
        pb = lambda name, shape: ctx.enter_context(nc.psum_tensor(name, shape, F32))
        sem = lambda name: ctx.enter_context(nc.semaphore(name))
        ident, cols, eps = keep["ident"], keep["cols"], keep["eps"]
        QK = 2 * E
        QKH = 2 * H
        HALF = D // 2

        wqkv = sb("wqkv", [P, KT, 3 * E])
        x_in = [sb(f"x_in{i}", [P, E]) for i in range(2)]
        rope = [sb(f"rope{i}", [P, 2, D]) for i in range(2)]
        x_stats = sb("x_stats", [P, 6])
        x_mv = sb("x_mv", [P, 2])
        x_std = sb("x_std", [P, 1])
        x_rstd = sb("x_rstd", [P, 1])
        xn = [sb(f"xn{i}", [P, E]) for i in range(2)]
        hT = [sb(f"hT{i}", [P, KT, P]) for i in range(2)]
        rot_cos = sb("rot_cos", [P, QKH, D])
        rot_sin = sb("rot_sin", [P, QKH, D])
        rot = sb("rot", [P, QKH, D])
        hsum = sb("hsum", [P, QKH])
        hmean = sb("hmean", [P, QKH])
        cent = [sb(f"cent{i}", [P, QKH, D]) for i in range(2)]
        csq = sb("csq", [P, QKH, D])
        hvar = sb("hvar", [P, QKH])
        hstd = sb("hstd", [P, QKH])
        hrstd = sb("hrstd", [P, QKH])
        qkn = sb("qkn", [P, QKH, D])
        qkT = sb("qkT", [P, QK])
        qk_round = [sb(f"qk_round{i}", [P, QK // P, P], F32R) for i in range(2)]
        qk_rest = [sb(f"qk_rest{i}", [P, QK // P, P], F32R) for i in range(2)]
        v_out = [sb(f"v_out{i}", [P, E]) for i in range(2)]

        xT_ps = pb("xT_ps", [P, KT, P])
        qk_ps = [pb(f"qk_ps{i}", [P, QKH, D]) for i in range(2)]
        v_ps = pb("v_ps", [P, E])
        qkT_ps = pb("qkT_ps", [P, QK])

        wqkv_loaded = sem("wqkv_loaded")
        x_loaded = [sem(f"x_loaded{i}") for i in range(2)]
        rope_loaded = [sem(f"rope_loaded{i}") for i in range(2)]
        xstat_done = sem("xstat_done")
        aggregate_open = sem("aggregate_open")
        xstd_done = sem("xstd_done")
        xrstd_done = sem("xrstd_done")
        xn_ready = sem("xn_ready")
        xT_ready = sem("xT_ready")
        hT_ready = sem("hT_ready")
        qk_summed = sem("qk_summed")
        v_summed = sem("v_summed")
        v_ready = sem("v_ready")
        parts_ready = sem("parts_ready")
        rot_ready = sem("rot_ready")
        hsum_done = sem("hsum_done")
        hmean_ready = sem("hmean_ready")
        cent_ready = sem("cent_ready")
        csq_ready = sem("csq_ready")
        hvar_ready = sem("hvar_ready")
        hstd_ready = sem("hstd_ready")
        hrstd_ready = sem("hrstd_ready")
        qkn_ready = sem("qkn_ready")
        turned = sem("turned")
        qkT_ready = sem("qkT_ready")
        round_ready = sem("round_ready")
        rest_ready = sem("rest_ready")
        round_stored = [sem(f"round_stored{i}") for i in range(2)]
        rest_stored = [sem(f"rest_stored{i}") for i in range(2)]
        v_stored = [sem(f"v_stored{i}") for i in range(2)]

        x_v = ins["x"].rearrange("o (t p) e -> (o t) p e", p=P)
        rope_v = ins["rope"].rearrange("(t p) a d -> t p a d", p=P)
        v_dst = v_scr.rearrange("(t p) e -> t p e", p=P)
        qk_dst = qk_scr.rearrange("a (c p) n -> a p c n", p=P)

        FIRST, PEELED, LAST = -2, 6, NB + 2

        def live(t):
            return not isinstance(t, int) or 0 <= t < NB

        def steps(eng, step):
            for s in range(FIRST, PEELED):
                step(s, s % 2)
            with eng.Fori(0, (NB - 2 - PEELED) // 2) as i:
                for b in range(2):
                    step(i * 2 + (PEELED + b), b)
            for s in range(NB - 2, LAST + 1):
                step(s, s % 2)

        def wait(eng, s, value):
            if not isinstance(value, int) or value > 0:
                eng.wait_ge(s, value)

        def dmas(t, par):
            return (t - par) * 8

        block = ctx.enter_context(nc.Block())

        @block.sync
        def _(sp):
            def step(s, par):
                if live(s + 2):
                    t = s + 2
                    wait(sp, xn_ready, t - 1)
                    sp.dma_start(x_in[par][:, :], x_v[t]).then_inc(x_loaded[par], 16)
                if isinstance(s, int) and s == -1:
                    for k in range(KT):
                        sp.dma_start(wqkv[:, k, :], ins["w_qkv"][k * P:(k + 1) * P, :]).then_inc(wqkv_loaded, 16)
                if live(s):
                    wait(sp, parts_ready, s - 1)
                    sp.dma_start(rope[par][:, :, :], rope_v[s]).then_inc(rope_loaded[par], 16)
                if live(s - 1):
                    wait(sp, v_ready, s)
                    sp.dma_start(v_dst[s - 1], v_out[1 - par][:, :]).then_inc(v_stored[1 - par], 16)
                if live(s - 3):
                    t, odd = s - 3, 1 - par
                    wait(sp, round_ready, t + 1)
                    sp.dma_start(qk_dst[0, :, :, bass.ts(t, P)], qk_round[odd][:, :, :].bitcast(F32)).then_inc(round_stored[odd], 16)
                    wait(sp, rest_ready, t + 1)
                    sp.dma_start(qk_dst[1, :, :, bass.ts(t, P)], qk_rest[odd][:, :, :].bitcast(F32)).then_inc(rest_stored[odd], 16)

            steps(sp, step)
            for par in range(2):
                sp.wait_ge(v_stored[par], NB // 2 * 16)
                sp.wait_ge(round_stored[par], NB // 2 * 16)
                sp.wait_ge(rest_stored[par], NB // 2 * 16)

        @block.tensor
        def _(pe):
            def step(s, par):
                if live(s + 1):
                    t = s + 1
                    wait(pe, xn_ready, t + 1)
                    wait(pe, hT_ready, t)
                    for k in range(KT):
                        mm = pe.transpose(xT_ps[:, k, :], xn[1 - par][:, k * P:(k + 1) * P], ident[:, :])
                    mm.then_inc(xT_ready, 1)
                if live(s - 3):
                    t = s - 3
                    wait(pe, qkn_ready, t + 1)
                    wait(pe, qkT_ready, t)
                    for c in range(QK // P):
                        mm = pe.transpose(qkT_ps[:, c * P:(c + 1) * P], qkn[:, c * HPG:(c + 1) * HPG, :], ident[:, :])
                    mm.then_inc(turned, 1)
                if live(s):
                    wait(pe, hT_ready, s + 1)
                    wait(pe, parts_ready, s - 1)
                    if isinstance(s, int) and s == 0:
                        pe.wait_ge(wqkv_loaded, KT * 16)
                    for c in range(2):
                        for k in range(KT):
                            mm = pe.matmul(qk_ps[par][:, c * H:(c + 1) * H, :], hT[par][:, k, :],
                                           wqkv[:, k, c * E:(c + 1) * E], start=(k == 0), stop=(k == KT - 1))
                    mm.then_inc(qk_summed, 1)
                    wait(pe, v_ready, s)
                    for k in range(KT):
                        mm = pe.matmul(v_ps[:, :], hT[par][:, k, :], wqkv[:, k, 2 * E:3 * E],
                                       start=(k == 0), stop=(k == KT - 1))
                    mm.then_inc(v_summed, 1)

            steps(pe, step)

        @block.vector
        def _(dve):
            def step(s, par):
                odd = 1 - par
                if live(s + 1):
                    t = s + 1
                    wait(dve, xT_ready, t + 1)
                    wait(dve, v_summed, t - 1)
                    for k in range(KT):
                        op = dve.tensor_scalar(hT[odd][:, k, :], xT_ps[:, k, :], cols[:, 1, k:k + 1],
                                               cols[:, 0, k:k + 1], ALU.mult, ALU.add)
                    op.then_inc(hT_ready, 1)
                if live(s - 1):
                    t = s - 1
                    wait(dve, qk_summed, t + 1)
                    wait(dve, rope_loaded[odd], dmas(t, odd) + 16)
                    wait(dve, rot_ready, t)
                    table = rope[odd]
                    dve.tensor_tensor(rot_cos[:, :, :], qk_ps[odd][:, :, :],
                                      table[:, 0:1, :].broadcast_to([P, QKH, D]), ALU.mult)
                    dve.tensor_tensor(rot_sin[:, :, 0:HALF], qk_ps[odd][:, :, HALF:D],
                                      table[:, 1:2, 0:HALF].broadcast_to([P, QKH, HALF]), ALU.mult)
                    dve.tensor_tensor(rot_sin[:, :, HALF:D], qk_ps[odd][:, :, 0:HALF],
                                      table[:, 1:2, HALF:D].broadcast_to([P, QKH, HALF]), ALU.mult).then_inc(parts_ready, 1)
                if live(s - 2):
                    t = s - 2
                    wait(dve, csq_ready, t + 1)
                    dve.tensor_reduce(hvar[:, :], csq[:, :, :], AX.X, ALU.add).then_inc(hvar_ready, 1)
                if live(s + 2):
                    t = s + 2
                    wait(dve, x_loaded[par], dmas(t, par) + 16)
                    wait(dve, xrstd_done, t)
                    dve.bn_stats(x_stats[:, :], x_in[par][:, :]).then_inc(xstat_done, 1)
                    wait(dve, xstat_done, t * 2 + 1)
                if live(s - 3):
                    t = s - 3
                    wait(dve, qkT_ready, t + 1)
                    wait(dve, round_stored[odd], dmas(t, odd))
                    dve.tensor_copy(qk_round[odd][:, :, :].rearrange("p c n -> p (c n)"), qkT[:, :]).then_inc(round_ready, 1)
                if live(s + 2):
                    wait(dve, xn_ready, s + 2)
                    dve.sem_inc(aggregate_open, 1)
                    dve.bn_aggr(x_mv[:, :], x_stats[:, :]).then_inc(xstat_done, 1)
                if live(s - 2):
                    t = s - 2
                    wait(dve, hstd_ready, t + 1)
                    dve.reciprocal(hrstd[:, :], hstd[:, :]).then_inc(hrstd_ready, 1)
                if live(s + 2):
                    t = s + 2
                    wait(dve, xstd_done, t + 1)
                    dve.reciprocal(x_rstd[:, :], x_std[:, :]).then_inc(xrstd_done, 1)
                if live(s - 2):
                    t = s - 2
                    wait(dve, hrstd_ready, t + 1)
                    wait(dve, turned, t)
                    dve.tensor_tensor(qkn[:, :, :], cent[par][:, :, :],
                                      hrstd[:, :].unsqueeze(2).broadcast_to([P, QKH, D]), ALU.mult).then_inc(qkn_ready, 1)
                if live(s + 2):
                    t = s + 2
                    wait(dve, xrstd_done, t + 1)
                    wait(dve, xT_ready, t - 1)
                    dve.tensor_scalar(xn[par][:, :], x_in[par][:, :], x_mv[:, 0:1], x_rstd[:, :],
                                      ALU.subtract, ALU.mult).then_inc(xn_ready, 1)
                if live(s - 1):
                    t = s - 1
                    wait(dve, rot_ready, t + 1)
                    dve.tensor_reduce(hsum[:, :], rot[:, :, :], AX.X, ALU.add).then_inc(hsum_done, 1)
                    wait(dve, hsum_done, t + 1)
                    wait(dve, cent_ready, t)
                    dve.tensor_scalar(hmean[:, :], hsum[:, :], 1.0 / D, None, ALU.mult).then_inc(hmean_ready, 1)

            steps(dve, step)

        @block.scalar
        def _(act):
            def step(s, par):
                odd = 1 - par
                if live(s - 2):
                    t = s - 2
                    wait(act, cent_ready, t + 1)
                    wait(act, hvar_ready, t)
                    act.activation(csq[:, :, :], cent[par][:, :, :], ACT.Square).then_inc(csq_ready, 1)
                if live(s - 3):
                    t = s - 3
                    wait(act, turned, t + 1)
                    wait(act, round_ready, t)
                    wait(act, rest_ready, t)
                    act.activation(qkT[:, :], qkT_ps[:, :], ACT.Identity, bias=keep["qk_bias"][:, :],
                                   scale=keep["qk_scale"][:, :]).then_inc(qkT_ready, 1)
                if live(s - 1):
                    t = s - 1
                    wait(act, v_summed, t + 1)
                    wait(act, v_stored[odd], dmas(t, odd))
                    act.activation(v_out[odd][:, :], v_ps[:, :], ACT.Copy).then_inc(v_ready, 1)
                if live(s - 2):
                    t = s - 2
                    wait(act, hvar_ready, t + 1)
                    act.activation(hstd[:, :], hvar[:, :], ACT.Sqrt, bias=eps[:, :], scale=1.0 / D).then_inc(hstd_ready, 1)
                if live(s + 2):
                    t = s + 2
                    wait(act, xstat_done, t * 2 + 2)
                    act.activation(x_std[:, :], x_mv[:, 1:2], ACT.Sqrt, bias=eps[:, :]).then_inc(xstd_done, 1)

            steps(act, step)

        @block.gpsimd
        def _(pool):
            def step(s, par):
                odd = 1 - par
                if live(s - 1):
                    t = s - 1
                    wait(pool, parts_ready, t + 1)
                    wait(pool, hsum_done, t)
                    wait(pool, cent_ready, t)
                    pool.tensor_tensor(rot[:, :, :], rot_cos[:, :, :], rot_sin[:, :, :], ALU.add).then_inc(rot_ready, 1)
                if live(s - 3):
                    t = s - 3
                    wait(pool, round_ready, t + 1)
                    wait(pool, rest_stored[odd], dmas(t, odd))
                    pool.tensor_tensor(qk_rest[odd][:, :, :].rearrange("p c n -> p (c n)"), qkT[:, :],
                                       qk_round[odd][:, :, :].rearrange("p c n -> p (c n)").bitcast(F32),
                                       ALU.subtract).then_inc(rest_ready, 1)
                if live(s - 1):
                    t = s - 1
                    wait(pool, hmean_ready, t + 1)
                    wait(pool, qkn_ready, t - 1)
                    wait(pool, csq_ready, t - 1)
                    pool.tensor_tensor(cent[odd][:, :, :], rot[:, :, :],
                                       hmean[:, :].unsqueeze(2).broadcast_to([P, QKH, D]), ALU.subtract).then_inc(cent_ready, 1)

            steps(pool, step)


def attention_phase(nc, keep, ins, qk_scr, v_scr, att_scr):
    with ExitStack() as ctx:
        sb = lambda name, shape, dt=F32: ctx.enter_context(nc.sbuf_tensor(name, shape, dt))
        sem = lambda name: ctx.enter_context(nc.semaphore(name))
        QBUF, SQBUF, POWBUF, SUMBUF, LAG = 2, 5, 12, 4, 5
        WEIGH_LAG = 2
        SUM_LAG = 2
        PAIR = 2
        HALVES = HPG // PAIR
        PIECES = 4
        PIECE = CHUNK // PIECES
        APART = 3

        k_stack = sb("k_stack", [P, HPG, N], F32R)
        v_grp = sb("v_grp", [P, NB, P])
        q_stack = [sb(f"q_stack{i}", [P, HPG, CHUNK], F32R) for i in range(QBUF)]
        squares = [sb(f"squares{i}", [P, PAIR, CHUNK]) for i in range(SQBUF)]
        powers = [sb(f"powers{i}", [P, PAIR, CHUNK]) for i in range(POWBUF)]
        sums = [sb(f"sums{i}", [P, PAIR, CHUNK]) for i in range(SUMBUF)]
        ones = sb("ones", [P, D])
        inv_den = sb("inv_den", [P, CHUNK])
        att = [sb(f"att{i}", [P, CHUNK]) for i in range(2)]
        weights = sb("weights", [P, KT, E])
        piece_max = sb("piece_max", [P, 3, NG * PIECES])
        own_max = sb("own_max", [P, 6])
        score_ps = [ctx.enter_context(nc.psum_tensor(f"score_ps{i}", [P, PAIR, CHUNK], F32)) for i in range(2)]
        num_ps = [ctx.enter_context(nc.psum_tensor(f"num_ps{i}", [P, CHUNK], F32)) for i in range(2)]
        den_ps = [ctx.enter_context(nc.psum_tensor(f"den_ps{i}", [P, CHUNK], F32)) for i in range(2)]

        k_loaded = [sem(f"k_loaded{c}") for c in range(NCH)]
        q_loaded = [sem(f"q_loaded{i}") for i in range(QBUF)]
        kv_free = sem("kv_free")
        q_free = sem("q_free")
        ones_ready = sem("ones_ready")
        scores_ready = sem("scores_ready")
        squares_ready = sem("squares_ready")
        masked_ready = sem("masked_ready")
        select_open = sem("select_open")
        dma_open = sem("dma_open")
        dve_powers = sem("dve_powers")
        act_powers = sem("act_powers")
        step_used = sem("step_used")
        sums_ready = sem("sums_ready")
        sums_used = sem("sums_used")
        inverse_ready = sem("inverse_ready")
        att_ready = sem("att_ready")
        att_stored = [sem(f"att_stored{i}") for i in range(2)]
        weights_loaded = sem("weights_loaded")
        surveyed = sem("surveyed")
        own_ready = sem("own_ready")
        sizes_ready = sem("sizes_ready")

        steps = [(j, i) for j in range(NCH) for i in range(BPC * (j + 1))]
        S = len(steps)
        U = HALVES * S
        diagonals = [u for u in range(U) if steps[u // HALVES][1] >= BPC * steps[u // HALVES][0]]
        chunk_end = [max(st for st in range(S) if steps[st][0] == j) for j in range(NCH)]
        last_use = {max(st for st in range(S) if steps[st][1] == BPC * c + BPC - 1): c for c in range(NCH)}
        pair_starts = [st for st, (j, i) in enumerate(steps) if i < BPC * j and i % 2 == 0 and i // 2 % 4 != 3]
        adds = [(st, half) for st in pair_starts for half in range(HALVES)]
        summed = {HALVES * (st + second) + half: n for n, (st, half) in enumerate(adds) for second in range(2)}
        by_act = [u for u in range(U) if u not in diagonals and u % 8 == 7]
        by_dve = [u for u in range(U) if u not in by_act]
        AP, DP, A = len(by_act), len(by_dve), len(adds)

        def den_items(s):
            direct = [("powers", s - WEIGH_LAG)] if s >= WEIGH_LAG and HALVES * (s - WEIGH_LAG) not in summed else []
            return direct + [("sum", st) for st in pair_starts if st + 1 + WEIGH_LAG + SUM_LAG == s]

        den_order = [[item for s in range(S + WEIGH_LAG) for item in den_items(s) if steps[item[1]][0] == j] for j in range(NCH)]

        def first_query(u):
            j, i = steps[u // HALVES]
            return max(0, i - BPC * j) * P

        def up_to(members, u):
            return sum(m <= u for m in members)

        def wait_powers(eng, g, u):
            if u in by_act:
                eng.wait_ge(act_powers, g * AP + (up_to(by_act, u) + START))
            else:
                eng.wait_ge(dve_powers, g * DP + (up_to(by_dve, u) + START))

        def wait_powers_free(eng, g, u):
            eng.wait_ge(step_used, g * S + (max(u - POWBUF + HALVES, 0) // HALVES + START))
            if u - POWBUF in summed:
                eng.wait_ge(sums_ready, g * A + (summed[u - POWBUF] + 1))

        k_src = qk_scr[:, E:2 * E, :].rearrange("a (g h d) n -> a g d h n", g=NG, h=HPG)
        q_src = qk_scr[:, 0:E, :].rearrange("a (g h d) n -> a g d h n", g=NG, h=HPG)
        v_src = v_scr.rearrange("(t p) (g e) -> g p t e", p=P, g=NG)
        att_dst = att_scr.rearrange("(g p) n -> g p n", g=NG)
        quarters = [ins[w].rearrange("(k p) (g n) -> g p k n", p=P, g=NG) for w in ("w_gate", "w_up")]
        quarters.append(ins["w_down"].rearrange("(g k p) n -> g p k n", p=P, g=NG))
        SURVEY_AT = (90, 150, 210)
        Q_PARTS = (0, 0, 1, 1)
        K_PARTS = (0, 1, 0, 1)
        KV_DMAS = len(K_PARTS) + 1
        block = ctx.enter_context(nc.Block())

        @block.sync
        def _(sp):
            with sp.Fori(0, NG) as g:
                for c in range(NCH):
                    sp.wait_ge(kv_free, g * NCH + (c + 1))
                    for a, part in enumerate(K_PARTS):
                        sp.dma_start(k_stack[a * D:(a + 1) * D, :, c * CHUNK:(c + 1) * CHUNK].bitcast(F32),
                                     k_src[part, g, :, :, c * CHUNK:(c + 1) * CHUNK]).then_inc(k_loaded[c], 16)
                    sp.dma_start(v_grp[:, c * BPC:(c + 1) * BPC, :],
                                 v_src[g, :, c * BPC:(c + 1) * BPC, :]).then_inc(k_loaded[c], 16)
                    sp.wait_ge(ones_ready, 1)
                    sp.wait_ge(q_free, g * NCH + (c + 1))
                    for a, part in enumerate(Q_PARTS):
                        sp.dma_start(q_stack[c % QBUF][a * D:(a + 1) * D, :, :].bitcast(F32),
                                     q_src[part, g, :, :, c * CHUNK:(c + 1) * CHUNK]).then_inc(q_loaded[c % QBUF], 16)

        @block.tensor
        def _(pe):
            pe.sem_inc(step_used, START)
            pe.sem_inc(sums_used, START)
            pe.sem_inc(kv_free, NCH)
            pe.sem_inc(q_free, QBUF)
            pe.wait_ge(ones_ready, 1)

            def scores(g, u):
                st, half = u // HALVES, u % HALVES
                j, i = steps[st]
                n0 = first_query(u)
                if i == 0 and half == 0:
                    pe.wait_ge(q_loaded[j % QBUF], (g * (NCH // QBUF) + (j // QBUF + 1)) * (16 * len(Q_PARTS)))
                if i == BPC * j and half == 0:
                    pe.wait_ge(k_loaded[j], (g + 1) * (16 * KV_DMAS))
                pe.wait_ge(squares_ready, g * U + (max(u - 1, 0) + START))
                for h in range(PAIR):
                    hh = half * PAIR + h
                    mm = pe.matmul(score_ps[u % 2][:, h, n0:], k_stack[:, hh, i * P:(i + 1) * P],
                                   q_stack[j % QBUF][:, hh, n0:], start=True, stop=True)
                    if half == 0 and h == 0 and st - WEIGH_LAG - 1 in last_use:
                        mm.then_inc(kv_free, 1)
                mm.then_inc(scores_ready, 1)

            def numerators(g, st):
                j, i = steps[st]
                n0 = first_query(HALVES * st)
                if i == 0:
                    pe.wait_ge(att_ready, g * NCH + (max(j - 1, 0) + START))
                for half in range(HALVES):
                    u = HALVES * st + half
                    wait_powers(pe, g, u)
                    for h in range(PAIR):
                        hh = half * PAIR + h
                        mm = pe.matmul(num_ps[j % 2][hh * D:(hh + 1) * D, n0:], v_grp[:, i, hh * D:(hh + 1) * D],
                                       powers[u % POWBUF][:, h, n0:], start=(i == 0), stop=(st == chunk_end[j]))
                        if hh == 0 and st in chunk_end:
                            mm.then_inc(q_free, 1)
                if HALVES * st in summed:
                    mm.then_inc(step_used, 1)

            def denominators(g, item):
                kind, st = item
                j = steps[st][0]
                n0 = first_query(HALVES * st)
                for hh in range(HPG):
                    half, h = hh // PAIR, hh % PAIR
                    if kind == "powers":
                        src = powers[(HALVES * st + half) % POWBUF]
                    else:
                        n = adds.index((st, half))
                        src = sums[n % SUMBUF]
                        if h == 0:
                            pe.wait_ge(sums_ready, g * A + (n + 1))
                    mm = pe.matmul(den_ps[j % 2][hh * D:(hh + 1) * D, n0:], ones[:, :], src[:, h, n0:],
                                   start=(item == den_order[j][0]), stop=(item == den_order[j][-1]))
                    if kind == "sum" and h == PAIR - 1:
                        mm.then_inc(sums_used, 1)
                    if st == S - 1 and hh == 0:
                        mm.then_inc(kv_free, 1)
                if kind == "powers":
                    mm.then_inc(step_used, 1)

            with pe.Fori(0, NG) as g:
                for s in range(S + WEIGH_LAG):
                    if s < S:
                        scores(g, HALVES * s)
                    if s >= WEIGH_LAG:
                        numerators(g, s - WEIGH_LAG)
                    if s < S:
                        scores(g, HALVES * s + 1)
                    for item in den_items(s):
                        denominators(g, item)

        @block.scalar
        def _(act):
            act.sem_inc(squares_ready, START)
            act.sem_inc(act_powers, START)
            with act.Fori(0, NG) as g:
                for u in range(U):
                    n0 = first_query(u)
                    act.wait_ge(scores_ready, g * U + (u + 1))
                    if u >= SQBUF:
                        wait_powers(act, g, u - SQBUF)
                    else:
                        act.wait_ge(dve_powers, g * DP + START)
                    act.activation(squares[u % SQBUF][:, :, n0:], score_ps[u % 2][:, :, n0:], ACT.Square).then_inc(squares_ready, 1)
                    if u - 1 in by_act:
                        m = u - 1
                        act.wait_ge(squares_ready, g * U + (m + 1 + START))
                        wait_powers_free(act, g, m)
                        act.activation(powers[m % POWBUF][:, :, :], squares[m % SQBUF][:, :, :], ACT.Square).then_inc(act_powers, 1)

        @block.gpsimd
        def _(pool):
            def select(g, u):
                n0 = first_query(u)
                pool.wait_ge(squares_ready, g * U + (u + 1 + START))
                pool.sem_inc(select_open, 1)
                corner = squares[u % SQBUF][:, :, n0:n0 + P]
                pool.affine_select(out=corner, in_=corner, compare_op=ALU.is_ge, fill=0.0, base=0,
                                   pattern=[[0, PAIR], [1, P]], channel_multiplier=-1).then_inc(masked_ready, 1)

            def add(g, n):
                st, half = adds[n]
                u = HALVES * st + half
                pool.wait_ge(sums_used, g * A + (max(n - SUMBUF + 1, 0) + START))
                wait_powers(pool, g, u)
                wait_powers(pool, g, u + HALVES)
                pool.tensor_tensor(sums[n % SUMBUF][:, :, :], powers[u % POWBUF][:, :, :],
                                   powers[(u + HALVES) % POWBUF][:, :, :], ALU.add).then_inc(sums_ready, 1)

            def store(g, j):
                pool.wait_ge(att_ready, g * NCH + (j + 1 + START))
                pool.sem_inc(dma_open, 1)
                pool.dma_start(att_dst[g, :, j * CHUNK:(j + 1) * CHUNK], att[j % 2][:, :]).then_inc(att_stored[j % 2], 16)

            def load_weights(g, t):
                pool.wait_ge(surveyed, g * (3 * PIECES) + (t * PIECES + START))
                pool.sem_inc(dma_open, 1)
                pool.dma_start(weights[:, :, :], quarters[t][g]).then_inc(weights_loaded, 16)

            events = [(u, select, u) for u in diagonals]
            events += [(HALVES * (adds[n][0] + 1) + adds[n][1] + 0.5, add, n) for n in range(A)]
            events += [(HALVES * chunk_end[j] + LAG + APART * PIECES + 4.5, store, j) for j in range(NCH)]
            events += [(at - 20.5, load_weights, t) for t, at in enumerate(SURVEY_AT)]
            events.sort(key=lambda event: event[0])
            with pool.Fori(0, NG) as g:
                for _, stage, n in events:
                    stage(g, n)
            pool.wait_ge(own_ready, 6)
            pool.partition_all_reduce(keep["sizes"][:, :], own_max[:, :], channels=P, reduce_op=RMAX).then_inc(sizes_ready, 1)
            for i in range(2):
                pool.wait_ge(att_stored[i], NG * NCH // 2 * 16)

        @block.vector
        def _(dve):
            dve.sem_inc(dve_powers, START)
            dve.sem_inc(att_ready, START)
            dve.sem_inc(surveyed, START)
            dve.memset(ones[:, :], 1.0).then_inc(ones_ready, 1)

            def normalise(g, j, p):
                part = slice(p * PIECE, (p + 1) * PIECE)
                dve.wait_ge(step_used, g * S + (chunk_end[j] + 1 + START))
                dve.reciprocal(inv_den[:, part], den_ps[j % 2][:, part]).then_inc(inverse_ready, 1)
                if p == PIECES - 1:
                    if j >= 2:
                        dve.wait_ge(att_stored[j % 2], (g * (NCH // 2) + j // 2) * 16)
                    dve.wait_ge(inverse_ready, (g * NCH + (j + 1)) * PIECES)
                    dve.tensor_tensor(att[j % 2][:, :], num_ps[j % 2][:, :], inv_den[:, :], ALU.mult).then_inc(att_ready, 1)

            def survey(g, t, p):
                dve.wait_ge(weights_loaded, (g * 3 + (t + 1)) * 16)
                dve.tensor_reduce(piece_max[:, t, bass.ts(g * PIECES + p, 1)], weights[:, p, :], axis=AX.X, op=ALU.max,
                                  apply_absolute_value=True).then_inc(surveyed, 1)

            with dve.Fori(0, NG) as g:
                for u in range(U):
                    n0 = first_query(u)
                    if u in by_dve:
                        if u in diagonals:
                            dve.wait_ge(masked_ready, g * len(diagonals) + (diagonals.index(u) + 1))
                        else:
                            dve.wait_ge(squares_ready, g * U + (u + 1 + START))
                        wait_powers_free(dve, g, u)
                        sq = squares[u % SQBUF][:, :, n0:]
                        dve.tensor_tensor(powers[u % POWBUF][:, :, n0:], sq, sq, ALU.mult).then_inc(dve_powers, 1)
                    for j in range(NCH):
                        after = u - (HALVES * chunk_end[j] + HALVES + LAG)
                        if after % APART == 0 and 0 <= after // APART < PIECES:
                            normalise(g, j, after // APART)
                    for t, at in enumerate(SURVEY_AT):
                        if (u - at) % APART == 0 and 0 <= (u - at) // APART < PIECES:
                            survey(g, t, (u - at) // APART)
                for p in range(PIECES):
                    normalise(g, NCH - 1, p)
                for i in range(2):
                    dve.wait_ge(att_stored[i], (g + 1) * (NCH // 2 * 16))
            dve.wait_ge(surveyed, 3 * PIECES * NG + START)
            for t in range(3):
                dve.tensor_reduce(own_max[:, t:t + 1], piece_max[:, t, :], axis=AX.X, op=ALU.max).then_inc(own_ready, 1)
            for t, src in ((3, keep["cols"][:, 3, :]), (4, keep["cols"][:, 2, :]), (5, keep["gate_b"][:, :])):
                dve.tensor_reduce(own_max[:, t:t + 1], src, axis=AX.X, op=ALU.max, apply_absolute_value=True).then_inc(own_ready, 1)


def mlp_phase(nc, keep, ins, att_scr, out):
    with ExitStack() as ctx:
        sb = lambda name, shape, dt=F32: ctx.enter_context(nc.sbuf_tensor(name, shape, dt))
        sem = lambda name: ctx.enter_context(nc.semaphore(name))
        ident, cols, eps, sizes = keep["ident"], keep["cols"], keep["eps"], keep["sizes"]
        PL = 4
        IC = INNER // (PL * P)
        KI = INNER // P
        PARTS = 2
        HALF = KT // 2
        FIRST_BANKS = (2, 3)
        LAST_BANKS = (0, 1)
        BANKS = FIRST_BANKS + LAST_BANKS
        PRODUCTS = ((0, 0), (0, 1), (1, 0))
        PPC = IC * PL
        TINY = 2.0 ** -30
        EXPONENT = 0x7F800000

        w_out = sb("w_out", [P, KT, E])
        w_gate = sb("w_gate", [P, PARTS, KT, IC, PL, P], F16)
        w_up = sb("w_up", [P, PARTS, KT, IC, PL, P], F16)
        w_down = sb("w_down", [P, PARTS, KI, E], F16)
        staged = [sb(f"staged{i}", [P, HALF, PL * P]) for i in range(2)]
        feed = sb("feed", [P, NG * CHUNK])
        att = feed[:, :].rearrange("p (g n) -> p g n", g=NG)
        xn = feed[:, :].rearrange("p (b e) -> p b e", b=BPC)
        x_mid = [sb(f"x_mid{i}", [P, BPC, E]) for i in range(2)]
        stats = sb("stats", [P, BPC, 6])
        mv = sb("mv", [P, BPC, 2])
        std = sb("std", [P, BPC])
        rstd = sb("rstd", [P, BPC])
        turned = sb("turned", [P, CHUNK])
        hT = [sb(f"hT_mid{i}", [P, PARTS, KT, CHUNK], F16) for i in range(2)]
        silu = [sb(f"silu{i}", [P, CHUNK]) for i in range(2)]
        hid = [sb(f"hid{i}", [P, PL, CHUNK]) for i in range(2)]
        size = sb("size", [P, PL, CHUNK])
        early = sb("early", [P, 3, CHUNK], BF16)
        late = sb("late", [P, 3, CHUNK], BF16)
        score = sb("score", [P, PL, CHUNK], BF16)
        kept = sb("kept", [P, PARTS, PL, CHUNK], F16)
        bound = sb("bound", [P, 4])
        power = sb("power", [P, 4])
        inverse = sb("inverse", [P, 4])
        scale = sb("scale", [P, 4])
        root = sb("root", [P, 2])
        kept_scale = sb("kept_scale", [P, 1])
        unscale = sb("unscale", [P, 3])
        shift_b = sb("shift_b", [P, KT])
        scale_b = sb("scale_b", [P, KT])
        ring = [ctx.enter_context(nc.psum_tensor(f"ring{i}", [P, E], F32)) for i in range(4)]
        y_ps = [ctx.enter_context(nc.psum_tensor(f"y_ps{i}", [P, E], F32)) for i in range(BPC)]

        w_out_loaded = sem("w_out_loaded")
        w_out_gated = sem("w_out_gated")
        staged_loaded = [sem(f"staged_loaded{i}") for i in range(2)]
        down_gated = sem("down_gated")
        w_high = sem("w_high")
        w_rest = sem("w_rest")
        scale_step = sem("scale_step")
        att_loaded = sem("att_loaded")
        x_loaded = [sem(f"xr_loaded{i}") for i in range(2)]
        projected = sem("projected")
        mid_ready = sem("mid_ready")
        stat_step = sem("stat_step")
        norm_open = sem("norm_open")
        std_ready = sem("std_ready")
        rstd_ready = sem("rstd_ready")
        xn_ready = sem("xnm_ready")
        xT_ready = sem("xTm_ready")
        turned_ready = sem("turned_ready")
        high_ready = sem("high_ready")
        hT_ready = sem("hTm_ready")
        pair_ready = sem("pair_ready")
        silu_ready = sem("silu_ready")
        hid_ready = sem("hid_ready")
        size_ready = sem("size_ready")
        early_ready = sem("early_ready")
        late_ready = sem("late_ready")
        part_ready = sem("part_ready")
        score_ready = sem("score_ready")
        select_ready = sem("select_ready")
        kept_high = sem("kept_high")
        kept_ready = sem("kept_ready")
        down_done = sem("down_done")
        y_ready = sem("y_ready")
        out_ready = sem("out_ready")
        out_stored = [sem(f"out_stored{i}") for i in range(2)]

        x_v = ins["x"].rearrange("o (c b p) e -> (o c) p b e", p=P, b=BPC)
        out_v = out.rearrange("o (c b p) e -> (o c) p b e", p=P, b=BPC)
        att_v = att_scr.rearrange("(g p) (c n) -> c p g n", p=P, n=CHUNK)
        gate_v = ins["w_gate"].rearrange("(k p) (i n) -> i p k n", p=P, i=IC)
        up_v = ins["w_up"].rearrange("(k p) (i n) -> i p k n", p=P, i=IC)
        down_v = ins["w_down"].rearrange("(i p a) e -> i p a e", p=P, a=PL)
        FIRST_STAGES = [(kind, 0, h) for kind in ("gate", "up") for h in range(2)]
        SLICE_STAGES = [[(kind, i + 1, h) for kind in ("gate", "up") for h in range(2) if i + 1 < IC] +
                        [("down", i, h) for h in range(2)] for i in range(IC)]
        STAGES = FIRST_STAGES + [stage for stages in SLICE_STAGES for stage in stages]
        SRC = {"gate": gate_v, "up": up_v, "down": down_v}

        def parts_up_to(kind, i):
            return STAGES.index((kind, i, 1)) + 1

        def chunks(eng, chunk):
            chunk(0, 0)
            with eng.Fori(0, (NCH - 2) // 2) as i:
                for b in range(2):
                    chunk(i * 2 + (1 + b), 1 - b)
            chunk(NCH - 1, (NCH - 1) % 2)

        def last(c):
            return isinstance(c, int) and c == NCH - 1

        def wait(eng, s, value):
            if not isinstance(value, int) or value > 0:
                eng.wait_ge(s, value)

        def dmas(c, par):
            return (c - par) * 8

        block = ctx.enter_context(nc.Block())

        @block.sync
        def _(sp):
            def load(c, par):
                wait(sp, out_stored[par], dmas(c, par))
                sp.dma_start(x_mid[par][:, :, :], x_v[c]).then_inc(x_loaded[par], 16)
                wait(sp, xT_ready, c * KT)
                sp.dma_start(att, att_v[c]).then_inc(att_loaded, 16)

            sp.dma_start(w_out[:, :, :], ins["w_out"].rearrange("(k p) e -> p k e", p=P)).then_inc(w_out_loaded, 16)
            load(0, 0)

            def chunk(c, par):
                if not (isinstance(c, int) and c == 0):
                    wait(sp, out_ready, c * BPC)
                    sp.dma_start(out_v[c - 1], x_mid[1 - par][:, :, :]).then_inc(out_stored[1 - par], 16)
                if not last(c):
                    load(c + 1, 1 - par)

            chunks(sp, chunk)
            sp.wait_ge(out_ready, NCH * BPC)
            sp.dma_start(out_v[NCH - 1], x_mid[(NCH - 1) % 2][:, :, :]).then_inc(out_stored[(NCH - 1) % 2], 16)
            for par in range(2):
                sp.wait_ge(out_stored[par], NCH // 2 * 16)

        @block.gpsimd
        def _(pool):
            for n, (kind, i, h) in enumerate(STAGES):
                if n >= 2:
                    pool.wait_ge(w_high, n - 1)
                    pool.wait_ge(w_rest, n - 1)
                pool.dma_start(staged[n % 2][:, :, :], SRC[kind][i][:, h * HALF:(h + 1) * HALF, :]).then_inc(staged_loaded[n % 2], 16)

        @block.tensor
        def _(pe):
            def project(c, banks):
                wait(pe, att_loaded, (c + 1) * 16)
                for b in banks:
                    if b == banks[0]:
                        wait(pe, hid_ready, (c - 1) * PPC + (2 * PL + 2 if banks == FIRST_BANKS else 2 * PL + 3))
                    for k in range(NG):
                        mm = pe.matmul(ring[b][:, :], att[:, k, b * P:(b + 1) * P], w_out[:, k, :],
                                       start=(k == 0), stop=(k == NG - 1))
                    mm.then_inc(projected, 1)

            def turn(c, banks):
                wait(pe, xn_ready, c * BPC + BPC)
                for k in banks:
                    if k == banks[0]:
                        wait(pe, hid_ready, (c - 1) * PPC + (3 * PL + 2 if banks == FIRST_BANKS else 3 * PL + 3))
                    for b in range(BPC):
                        mm = pe.transpose(ring[k][:, b * P:(b + 1) * P], xn[:, b, k * P:(k + 1) * P], ident[:, :])
                    mm.then_inc(xT_ready, 1)

            def gate_up(c, par, n):
                i, a = n // PL, n % PL
                if isinstance(c, int) and c == 0 and a == 0:
                    pe.wait_ge(w_rest, parts_up_to("up", i))
                    pe.wait_ge(w_high, parts_up_to("up", i))
                if n == 0:
                    wait(pe, hT_ready, (c + 1) * KT)
                if n in (2 * PL + 3, 2 * PL + 4) and not last(c):
                    wait(pe, mid_ready, (c + 1) * BPC + 2 * (n - 2 * PL - 2))
                elif n == 3 * PL + 3 and not last(c):
                    wait(pe, turned_ready, (c + 1) * KT + 2)
                else:
                    wait(pe, hid_ready, c * PPC + (n - 1))
                for w, bank in ((w_gate, ring[2 * (n % 2)]), (w_up, ring[2 * (n % 2) + 1])):
                    for k in range(KT):
                        for m, (wp, hp) in enumerate(PRODUCTS):
                            mm = pe.matmul(bank[:, :], w[:, wp, k, i, a, :], hT[par][:, hp, k, :],
                                           start=(k == 0 and m == 0), stop=(k == KT - 1 and m == 2))
                mm.then_inc(pair_ready, 1)

            def down(c, i):
                if isinstance(c, int) and c == 0:
                    pe.wait_ge(w_rest, parts_up_to("down", i))
                    pe.wait_ge(w_high, parts_up_to("down", i))
                wait(pe, kept_ready, c * IC + (i + 1))
                if i == 0:
                    wait(pe, out_ready, c * BPC)
                for b in range(BPC):
                    for a in range(PL):
                        for m, (kp, wp) in enumerate(PRODUCTS):
                            mm = pe.matmul(y_ps[b][:, :], kept[:, kp, a, b * P:(b + 1) * P],
                                           w_down[:, wp, i * PL + a, :], start=(i == 0 and a == 0 and m == 0),
                                           stop=(i == IC - 1 and a == PL - 1 and m == 2))
                    if b < BPC - 1:
                        if i == IC - 1:
                            mm.then_inc(y_ready, 1)
                    elif i < IC - 1:
                        mm.then_inc(down_done, 1)
                    else:
                        mm.then_inc(y_ready, 1)

            pe.wait_ge(w_out_gated, 1)
            project(0, BANKS)
            turn(0, BANKS)

            def chunk(c, par):
                for i in range(IC):
                    for a in range(PL - 1):
                        gate_up(c, par, i * PL + a)
                    if i == 2 and not last(c):
                        project(c + 1, FIRST_BANKS)
                    if i == 3 and not last(c):
                        turn(c + 1, FIRST_BANKS)
                    if i > 0:
                        down(c, i - 1)
                    elif not (isinstance(c, int) and c == 0):
                        down(c - 1, IC - 1)
                    if i == 2 and not last(c):
                        project(c + 1, LAST_BANKS)
                    if i == 3 and not last(c):
                        turn(c + 1, LAST_BANKS)
                    gate_up(c, par, i * PL + PL - 1)

            chunks(pe, chunk)
            down(NCH - 1, IC - 1)

        @block.scalar
        def _(act):
            def high(n):
                kind, i, h = STAGES[n]
                if kind == "down":
                    act.wait_ge(down_gated, 2 * i + h + 1)
                    at = i * PL + h * HALF
                    act.activation(w_down[:, 0, at:at + HALF, :], staged[n % 2][:, :, :], ACT.Copy).then_inc(w_high, 1)
                    return
                act.wait_ge(staged_loaded[n % 2], (n // 2 + 1) * 16)
                act.wait_ge(scale_step, SCALE_STEPS)
                w, which = (w_gate, 0) if kind == "gate" else (w_up, 1)
                for k in range(HALF):
                    op = act.activation(w[:, 0, h * HALF + k, i, :, :], staged[n % 2][:, k, :].rearrange("p (c a) -> p a c", a=PL),
                                        ACT.Identity, bias=0.0, scale=scale[:, which:which + 1])
                op.then_inc(w_high, 1)

            def deviation(c):
                wait(act, stat_step, c * (2 * BPC) + 2 * BPC)
                act.activation(std[:, :], mv[:, :, 1], ACT.Sqrt, bias=eps[:, :]).then_inc(std_ready, 1)

            def absolute(c, i, a):
                s = c * IC + i
                wait(act, hid_ready, s * PL + (a + 1))
                if a == 0:
                    wait(act, late_ready, s)
                act.activation(size[:, a, :], hid[i % 2][:, a, :], ACT.Abs).then_inc(size_ready, 1)

            def kept_parts(c, i):
                s = c * IC + i
                for a in range(PL):
                    wait(act, select_ready, s * PL + (a + 1))
                    if a == 0:
                        if i > 0:
                            wait(act, down_done, c * (IC - 1) + i)
                        else:
                            wait(act, y_ready, c * BPC)
                    act.activation(kept[:, 0, a, :], hid[i % 2][:, a, :], ACT.Copy).then_inc(kept_high, 1)

            SCALE_STEPS = 13
            deviation(0)
            for n in range(len(FIRST_STAGES)):
                high(n)

            def chunk(c, par):
                for i in range(IC):
                    for a in range(PL):
                        n = i * PL + a
                        wait(act, pair_ready, c * PPC + (n + 1))
                        wait(act, hid_ready, c * PPC + (n - 1))
                        act.activation(silu[n % 2][:, :], ring[2 * (n % 2)][:, :], ACT.Silu,
                                       scale=unscale[:, 0:1]).then_inc(silu_ready, 1)
                        absolute(c, i, a)
                        if a == 0 and i > 0:
                            kept_parts(c, i - 1)
                        elif a == 0 and not (isinstance(c, int) and c == 0):
                            kept_parts(c - 1, IC - 1)
                        if a == PL - 2 and isinstance(c, int) and c == 0:
                            for stage in SLICE_STAGES[i]:
                                high(STAGES.index(stage))
                        if a == PL - 2 and i == 2 and not last(c):
                            deviation(c + 1)

            chunks(act, chunk)
            kept_parts(NCH - 1, IC - 1)

        @block.vector
        def _(dve):
            steps = [0]

            def chained(op):
                steps[0] += 1
                op.then_inc(scale_step, 1)
                dve.wait_ge(scale_step, steps[0])

            dve.wait_ge(w_out_loaded, 16)
            for k in range(KT):
                op = dve.tensor_tensor(w_out[:, k, :], w_out[:, k, :], keep["gate_a"][:, :], ALU.mult)
            op.then_inc(w_out_gated, 1)
            ROOT_E = float(E) ** 0.5
            chained(dve.tensor_copy(bound[:, 0:2], sizes[:, 0:2]))
            chained(dve.tensor_tensor(bound[:, 2:3], sizes[:, 2:3], sizes[:, 5:6], ALU.mult))
            chained(dve.tensor_tensor(bound[:, 3:4], sizes[:, 3:4], sizes[:, 4:5], ALU.add))
            chained(dve.tensor_scalar(bound[:, 3:4], bound[:, 3:4], ROOT_E * 1.01, None, ALU.mult))
            chained(dve.tensor_scalar(bound[:, :], bound[:, :], TINY, None, ALU.max))
            chained(dve.tensor_scalar(power[:, :].bitcast(I32), bound[:, :].bitcast(I32), EXPONENT, None, ALU.bitwise_and))
            chained(dve.reciprocal(inverse[:, :], power[:, :]))
            chained(dve.tensor_scalar(scale[:, 0:4], inverse[:, 0:4], 2.0 ** 13, None, ALU.mult))
            chained(dve.tensor_scalar(root[:, :], inverse[:, 0:2], inverse[:, 3:4], 2.0, ALU.mult, ALU.mult))
            chained(dve.tensor_tensor(kept_scale[:, :], root[:, 0:1], root[:, 1:2], ALU.mult))
            chained(dve.reciprocal(unscale[:, 2:3], kept_scale[:, :]))
            chained(dve.tensor_scalar(unscale[:, 0:2], power[:, 0:2], power[:, 3:4], 2.0 ** -26, ALU.mult, ALU.mult))
            chained(dve.tensor_scalar(unscale[:, 2:3], unscale[:, 2:3], power[:, 2:3], 2.0 ** -13, ALU.mult, ALU.mult))
            dve.tensor_scalar(unscale[:, 1:2], unscale[:, 1:2], kept_scale[:, :], None, ALU.mult).then_inc(scale_step, 1)
            dve.tensor_scalar(shift_b[:, :], cols[:, 2, :], scale[:, 3:4], None, ALU.mult).then_inc(scale_step, 1)
            dve.tensor_scalar(scale_b[:, :], cols[:, 3, :], scale[:, 3:4], None, ALU.mult).then_inc(scale_step, 1)
            steps[0] += 3

            def rest(n):
                kind, i, h = STAGES[n]
                dve.wait_ge(staged_loaded[n % 2], (n // 2 + 1) * 16)
                if kind == "down":
                    for a in range(HALF):
                        op = dve.scalar_tensor_tensor(out=staged[n % 2][:, a, :], in0=staged[n % 2][:, a, :], scalar=scale[:, 2:3],
                                                      in1=keep["gate_b"][:, :], op0=ALU.mult, op1=ALU.mult)
                    op.then_inc(down_gated, 1)
                    at = i * PL + h * HALF
                    dve.wait_ge(w_high, n + 1)
                    dve.tensor_tensor(w_down[:, 1, at:at + HALF, :], staged[n % 2][:, :, :],
                                      w_down[:, 0, at:at + HALF, :], ALU.subtract).then_inc(w_rest, 1)
                    return
                w, which = (w_gate, 0) if kind == "gate" else (w_up, 1)
                dve.wait_ge(w_high, n + 1)
                for k in range(HALF):
                    row = h * HALF + k
                    op = dve.scalar_tensor_tensor(out=w[:, 1, row, i, :, :], in0=staged[n % 2][:, k, :].rearrange("p (c a) -> p a c", a=PL),
                                                  scalar=scale[:, which:which + 1], in1=w[:, 0, row, i, :, :],
                                                  op0=ALU.mult, op1=ALU.subtract)
                op.then_inc(w_rest, 1)

            def norm(c, par):
                wait(dve, x_loaded[par], dmas(c, par) + 16)
                for n, b in enumerate(BANKS):
                    wait(dve, projected, c * BPC + (n + 1))
                    dve.tensor_tensor(x_mid[par][:, b, :], ring[b][:, :], x_mid[par][:, b, :], ALU.add).then_inc(mid_ready, 1)
                    wait(dve, mid_ready, c * BPC + (n + 1))
                    dve.bn_stats(stats[:, b, :], x_mid[par][:, b, :]).then_inc(stat_step, 1)
                wait(dve, stat_step, c * (2 * BPC) + BPC)
                dve.sem_inc(norm_open, 1)
                for b in range(BPC):
                    dve.bn_aggr(mv[:, b, :], stats[:, b, :]).then_inc(stat_step, 1)
                wait(dve, std_ready, c + 1)
                dve.reciprocal(rstd[:, :], std[:, :]).then_inc(rstd_ready, 1)
                wait(dve, rstd_ready, c + 1)
                for b in range(BPC):
                    dve.tensor_scalar(xn[:, b, :], x_mid[par][:, b, :], mv[:, b, 0:1], rstd[:, b:b + 1],
                                      ALU.subtract, ALU.mult).then_inc(xn_ready, 1)

            def modulate(c, par):
                for n, k in enumerate(BANKS):
                    wait(dve, xT_ready, c * KT + (n + 1))
                    wait(dve, hT_ready, c * KT + n)
                    dve.tensor_scalar(turned[:, :], ring[k][:, :], scale_b[:, k:k + 1], shift_b[:, k:k + 1],
                                      ALU.mult, ALU.add).then_inc(turned_ready, 1)
                    wait(dve, turned_ready, c * KT + (n + 1))
                    dve.tensor_copy(hT[par][:, 0, k, :], turned[:, :]).then_inc(high_ready, 1)
                    wait(dve, high_ready, c * KT + (n + 1))
                    dve.tensor_tensor(hT[par][:, 1, k, :], turned[:, :], hT[par][:, 0, k, :], ALU.subtract).then_inc(hT_ready, 1)

            def hidden(c, i, a):
                s, n = c * IC + i, i * PL + a
                if a == 0:
                    wait(dve, kept_ready, s - 1)
                    wait(dve, size_ready, (s - 1) * PL)
                wait(dve, silu_ready, s * PL + (a + 1))
                dve.scalar_tensor_tensor(out=hid[i % 2][:, a, :], in0=ring[2 * (n % 2) + 1][:, :], scalar=unscale[:, 1:2],
                                         in1=silu[n % 2][:, :], op0=ALU.mult, op1=ALU.mult).then_inc(hid_ready, 1)


            def compare_early(c, i):
                s = c * IC + i
                wait(dve, size_ready, s * PL + 3)
                wait(dve, select_ready, s * PL)
                dve.tensor_tensor(early[:, 0, :], size[:, 0, :], size[:, 1, :], ALU.is_ge).then_inc(early_ready, 1)
                dve.tensor_tensor(early[:, 1:3, :], size[:, 0:2, :], size[:, 2:3, :].broadcast_to([P, 2, CHUNK]), ALU.is_ge).then_inc(early_ready, 1)
                wait(dve, early_ready, s * 2 + 2)
                dve.tensor_tensor(score[:, 0, :], early[:, 0, :], early[:, 1, :], ALU.add).then_inc(part_ready, 1)
                dve.tensor_tensor(score[:, 1, :], early[:, 2, :], early[:, 0, :], ALU.subtract).then_inc(part_ready, 1)
                dve.tensor_tensor(score[:, 2, :], early[:, 1, :], early[:, 2, :], ALU.add).then_inc(part_ready, 1)

            def compare_late(c, i):
                s = c * IC + i
                wait(dve, size_ready, s * PL + PL)
                dve.tensor_tensor(late[:, :, :], size[:, 0:3, :], size[:, 3:4, :].broadcast_to([P, 3, CHUNK]), ALU.is_ge).then_inc(late_ready, 1)
                wait(dve, late_ready, s + 1)
                wait(dve, part_ready, s * 4 + 3)
                dve.tensor_tensor(score[:, 3, :], late[:, 0, :], late[:, 1, :], ALU.add).then_inc(part_ready, 1)
                dve.tensor_tensor(score[:, 0:2, :], score[:, 0:2, :], late[:, 0:2, :], ALU.add).then_inc(score_ready, 1)
                dve.tensor_tensor(score[:, 2, :], late[:, 2, :], score[:, 2, :], ALU.subtract).then_inc(score_ready, 1)
                wait(dve, part_ready, s * 4 + 4)
                dve.tensor_tensor(score[:, 3, :], score[:, 3, :], late[:, 2, :], ALU.add).then_inc(score_ready, 1)

            def select(c, i):
                s = c * IC + i
                here = hid[i % 2]
                wait(dve, score_ready, s * 3 + 3)
                for a, (test, least) in enumerate(((ALU.is_ge, 2.0), (ALU.is_ge, 1.0), (ALU.is_ge, 0.0), (ALU.is_le, 1.0))):
                    dve.scalar_tensor_tensor(out=here[:, a, :], in0=score[:, a, :], scalar=least,
                                             in1=here[:, a, :], op0=test, op1=ALU.mult).then_inc(select_ready, 1)
                for b in range(2):
                    wait(dve, kept_high, s * PL + 2 * (b + 1))
                    op = dve.tensor_tensor(kept[:, 1, 2 * b:2 * b + 2, :], here[:, 2 * b:2 * b + 2, :],
                                           kept[:, 0, 2 * b:2 * b + 2, :], ALU.subtract)
                op.then_inc(kept_ready, 1)

            def add(c, par):
                for b in range(BPC):
                    wait(dve, y_ready, c * BPC + (b + 1))
                    dve.scalar_tensor_tensor(out=x_mid[par][:, b, :], in0=y_ps[b][:, :], scalar=unscale[:, 2:3],
                                             in1=x_mid[par][:, b, :], op0=ALU.mult, op1=ALU.add).then_inc(out_ready, 1)

            norm(0, 0)
            rest(0)
            rest(1)
            dve.wait_ge(scale_step, steps[0])
            modulate(0, 0)
            rest(2)
            rest(3)

            def chunk(c, par):
                for i in range(IC):
                    hidden(c, i, 0)
                    if i > 0:
                        select(c, i - 1)
                    elif not (isinstance(c, int) and c == 0):
                        select(c - 1, IC - 1)
                    hidden(c, i, 1)
                    hidden(c, i, 2)
                    compare_early(c, i)
                    if isinstance(c, int) and c == 0:
                        for stage in SLICE_STAGES[i]:
                            rest(STAGES.index(stage))
                    elif i == 0:
                        add(c - 1, 1 - par)
                    if i == 2 and not last(c):
                        norm(c + 1, 1 - par)
                    if i == 3 and not last(c):
                        modulate(c + 1, 1 - par)
                    hidden(c, i, 3)
                    compare_late(c, i)

            chunks(dve, chunk)
            select(NCH - 1, IC - 1)
            add(NCH - 1, (NCH - 1) % 2)


def adaln_kernel(nc, ins, out):
    qk_scr = nc.dram_tensor("qk_scr", [2, 2 * E, N], F32).ap()
    v_scr = nc.dram_tensor("v_scr", [N, E], F32).ap()
    att_scr = nc.dram_tensor("att_scr", [E, N], F32).ap()
    with ExitStack() as ctx:
        sb = lambda name, shape: ctx.enter_context(nc.sbuf_tensor(name, shape, F32))
        keep = {
            "ident": sb("ident", [P, P]),
            "gate_a": sb("gate_a", [P, E]),
            "gate_b": sb("gate_b", [P, E]),
            "cols": sb("cols", [P, 4, KT]),
            "qk_scale": sb("qk_scale", [P, 1]),
            "qk_bias": sb("qk_bias", [P, 1]),
            "eps": sb("eps", [P, 1]),
            "sizes": sb("sizes", [P, 6]),
        }
        setup_phase(nc, keep, ins)
        projection_phase(nc, keep, ins, qk_scr, v_scr)
        attention_phase(nc, keep, ins, qk_scr, v_scr, att_scr)
        mlp_phase(nc, keep, ins, att_scr, out)


_INS = {
    "x": "L0_attn_x", "w_qkv": "L0_attn_w_qkv", "w_out": "L0_attn_w_out", "ln_scale": "L0_attn_ln_scale",
    "ln_bias": "L0_attn_ln_bias", "w_gate": "L0_ffn_w_gate", "w_up": "L0_ffn_w_up", "w_down": "L0_ffn_w_down",
    "c": "L0_c", "wmod": "L0_wmod",
}


def rope_table():
    inv_freq = np.float32(1.0) / np.power(np.float32(ROPE_BASE), np.arange(0, D, 2, dtype=np.float32) / np.float32(D))
    angle = (np.arange(N, dtype=np.float32)[:, None] * inv_freq[None, :]).astype(np.float64)
    cos, sin = np.cos(angle), np.sin(angle)
    table = np.stack([np.concatenate([cos, cos], 1), np.concatenate([-sin, sin], 1)], 1)
    return table.astype(np.float32)


def kernel(**inputs):
    import concourse.bacc as _bacc
    from concourse.bass_utils import run_bass_kernel_spmd as _run

    nc = _bacc.Bacc("TRN2", target_bir_lowering=False, num_devices=1)
    arrays = {f"in_{short}": np.ascontiguousarray(inputs[name]) for short, name in _INS.items()}
    arrays["in_rope"] = rope_table()
    ins = {name[3:]: nc.dram_tensor(name, a.shape, mybir.dt.from_np(a.dtype), kind="ExternalInput").ap()
           for name, a in arrays.items()}
    out = nc.dram_tensor("out", (1, N, E), F32, kind="ExternalOutput").ap()
    adaln_kernel(nc, ins, out)
    r = _run(nc, [arrays], core_ids=[0])
    return r.results[0]["out"]
```

```python
from contextlib import ExitStack

import numpy as np

import concourse.bass as bass
from concourse import mybir

F32 = mybir.dt.float32
F32R = mybir.dt.float32r
BF16 = mybir.dt.bfloat16
F16 = mybir.dt.float16
I32 = mybir.dt.int32
ALU = mybir.AluOpType
ACT = mybir.ActivationFunctionType
AX = mybir.AxisListType
RMAX = bass.bass_isa.ReduceOp.max

P = 128
N = 4096
E = 512
H = 16
D = E // H
INNER = 2048
KT = E // P
NB = N // P
CHUNK = 512
NCH = N // CHUNK
BPC = CHUNK // P
HPG = P // D
NG = H // HPG
EPS = 1e-5
Q_PARTS = (0, 0, 1, 1)
K_PARTS = (0, 1, 0, 1)
ROPE_BASE = 10000.0


def setup_phase(nc, keep, w_parts, ins):
    with ExitStack() as ctx:
        sb = lambda name, shape, dt=F32: ctx.enter_context(nc.sbuf_tensor(name, shape, dt))
        sem = lambda name: ctx.enter_context(nc.semaphore(name))
        ident, gate_a, gate_b, cols = keep["ident"], keep["gate_a"], keep["gate_b"], keep["cols"]

        c_col = sb("c_col", [P, KT])
        silu_c = sb("silu_c", [P, KT])
        silu_wide = sb("silu_wide", [P, KT, P])
        wmod = sb("wmod", [P, KT, 6 * E])
        mod = sb("mod", [P, 6, E])
        gate_abs = sb("gate_abs", [P, 2, E])
        gate_neg = sb("gate_neg", [P, 2, E])
        gate_sign = sb("gate_sign", [P, 2, E])
        picked = sb("picked", [P, 4 * KT, P])
        wqkv = sb("wqkv", [P, KT, 3 * E])
        mod_ps = [ctx.enter_context(nc.psum_tensor(f"mod_ps{s}", [P, E], F32)) for s in range(6)]

        c_loaded = sem("c_loaded")
        wmod_loaded = [sem(f"wmod_loaded{s}") for s in range(6)]
        ident_zero = sem("ident_zero")
        ident_ready = sem("ident_ready")
        silu_done = sem("silu_done")
        wide_done = sem("wide_done")
        mod_summed = sem("mod_summed")
        mod_copied = sem("mod_copied")
        gate_step = sem("gate_step")
        cols_loaded = sem("cols_loaded")
        wqkv_loaded = [sem(f"wqkv_loaded{k}") for k in range(KT)]
        wqkv_rounded = sem("wqkv_rounded")

        wmod_v = ins["wmod"].rearrange("(k p) n -> p k n", p=P)
        block = ctx.enter_context(nc.Block())

        @block.sync
        def _(sp):
            sp.dma_start(c_col[:, :], ins["c"].rearrange("o (k p) -> p (o k)", p=P), allow_slow_non_contiguous=True).then_inc(c_loaded, 16)
            for s in range(6):
                sp.dma_start(wmod[:, :, s * E:(s + 1) * E], wmod_v[:, :, s * E:(s + 1) * E]).then_inc(wmod_loaded[s], 16)
                if s == 1:
                    for k in range(KT):
                        sp.dma_start(wqkv[:, k, :], ins["w_qkv"][k * P:(k + 1) * P, :]).then_inc(wqkv_loaded[k], 16)
            for h in range(HPG):
                sp.dma_start(keep["qk_scale"][h * D:(h + 1) * D, :], ins["ln_scale"].unsqueeze(1)).then_inc(cols_loaded, 16)
                sp.dma_start(keep["qk_bias"][h * D:(h + 1) * D, :], ins["ln_bias"].unsqueeze(1)).then_inc(cols_loaded, 16)
            sp.wait_ge(cols_loaded, 2 * HPG * 16)

        @block.gpsimd
        def _(pool):
            pool.memset(ident[:, :], 0.0).then_inc(ident_zero, 1)
            pool.wait_ge(ident_zero, 1)
            pool.affine_select(out=ident[:, :], in_=ident[:, :], compare_op=ALU.not_equal, fill=1.0,
                               base=0, pattern=[[-1, P]], channel_multiplier=1).then_inc(ident_ready, 1)
            for k in range(0, KT, 2):
                pool.wait_ge(wqkv_rounded, k + 1)
                pool.tensor_tensor(w_parts[1][:, k, :], wqkv[:, k, :], w_parts[0][:, k, :].bitcast(F32), ALU.subtract)

        @block.scalar
        def _(act):
            act.wait_ge(c_loaded, 16)
            act.activation(silu_c[:, :], c_col[:, :], ACT.Silu).then_inc(silu_done, 1)
            act.wait_ge(silu_done, 1)
            for k in range(KT):
                wide = act.activation(silu_wide[:, k, :], silu_c[:, k:k + 1].broadcast_to([P, P]), ACT.Copy)
            wide.then_inc(wide_done, 1)
            for s in range(6):
                act.wait_ge(mod_summed, s + 1)
                act.activation(mod[:, s, :], mod_ps[s][:, :], ACT.Copy).then_inc(mod_copied, 1)
                if s < KT:
                    act.wait_ge(wqkv_loaded[s], 16)
                    act.activation(w_parts[0][:, s, :], wqkv[:, s, :], ACT.Copy).then_inc(wqkv_rounded, 1)

        @block.tensor
        def _(pe):
            pe.wait_ge(wide_done, 1)
            for s in range(6):
                pe.wait_ge(wmod_loaded[s], 16)
                for k in range(KT):
                    mm = pe.matmul(mod_ps[s][:, :], silu_wide[:, k, :], wmod[:, k, s * E:(s + 1) * E],
                                   start=(k == 0), stop=(k == KT - 1))
                mm.then_inc(mod_summed, 1)

        @block.vector
        def _(dve):
            dve.memset(keep["eps"][:, :], EPS)
            dve.wait_ge(ident_ready, 1)
            for n, s in enumerate((0, 1, 3, 4)):
                dve.wait_ge(mod_copied, s + 1)
                for k in range(KT):
                    dve.scalar_tensor_tensor(
                        out=picked[:, n * KT + k, :], in0=mod[:, s, k * P:(k + 1) * P], scalar=1.0 if s in (1, 4) else 0.0,
                        in1=ident[:, :], op0=ALU.add, op1=ALU.mult, accum_out=cols[:, n, k:k + 1])
                if n % 2 == 1:
                    dve.wait_ge(wqkv_rounded, n + 1)
                    dve.tensor_tensor(w_parts[1][:, n, :], wqkv[:, n, :], w_parts[0][:, n, :].bitcast(F32), ALU.subtract)
            steps = 0
            for n, (s, gate) in enumerate(((2, gate_a), (5, gate_b))):
                dve.wait_ge(mod_copied, s + 1)
                dve.scalar_tensor_tensor(out=gate_neg[:, n, :], in0=mod[:, s, :], scalar=-1.0, in1=mod[:, s, :],
                                         op0=ALU.mult, op1=ALU.max).then_inc(gate_step, 1)
                dve.tensor_scalar(gate_sign[:, n, :], mod[:, s, :], 0.0, 2.0, ALU.is_ge, ALU.mult).then_inc(gate_step, 1)
                dve.wait_ge(gate_step, steps + 2)
                dve.tensor_scalar(gate_abs[:, n, :], gate_neg[:, n, :], 0.25, None, ALU.max).then_inc(gate_step, 1)
                dve.wait_ge(gate_step, steps + 3)
                dve.scalar_tensor_tensor(out=gate[:, :], in0=gate_sign[:, n, :], scalar=-1.0, in1=gate_abs[:, n, :],
                                         op0=ALU.add, op1=ALU.mult).then_inc(gate_step, 1)
                steps += 4


def projection_phase(nc, keep, w_parts, first_k, first_q, ins, qk_scr, v_scr):
    with ExitStack() as ctx:
        sb = lambda name, shape, dt=F32: ctx.enter_context(nc.sbuf_tensor(name, shape, dt))
        pb = lambda name, shape: ctx.enter_context(nc.psum_tensor(name, shape, F32))
        sem = lambda name: ctx.enter_context(nc.semaphore(name))
        ident, cols, eps = keep["ident"], keep["cols"], keep["eps"]
        QK = 2 * E
        QKH = 2 * H
        HALF = D // 2

        PRODUCTS = ((0, 0), (0, 1), (1, 0))
        x_in = [sb(f"x_in{i}", [P, E]) for i in range(2)]
        rope = [sb(f"rope{i}", [P, 2, D]) for i in range(2)]
        x_stats = sb("x_stats", [P, 6])
        x_mv = sb("x_mv", [P, 2])
        x_std = sb("x_std", [P, 1])
        x_rstd = sb("x_rstd", [P, 1])
        xn = [sb(f"xn{i}", [P, E]) for i in range(2)]
        hT = sb("hT", [P, KT, P])
        hT_parts = [[sb(f"hT_{part}{i}", [P, KT, P], F32R) for part in ("round", "rest")] for i in range(2)]
        rot_cos = sb("rot_cos", [P, QKH, D])
        rot_sin = sb("rot_sin", [P, QKH, D])
        rot = sb("rot", [P, QKH, D])
        hsum = sb("hsum", [P, QKH])
        hmean = sb("hmean", [P, QKH])
        cent = [sb(f"cent{i}", [P, QKH, D]) for i in range(2)]
        csq = sb("csq", [P, QKH, D])
        hvar = sb("hvar", [P, QKH])
        hstd = sb("hstd", [P, QKH])
        hrstd = sb("hrstd", [P, QKH])
        qkn = sb("qkn", [P, QKH, D])
        qkT = sb("qkT", [P, QK])
        qk_round = [sb(f"qk_round{i}", [P, QK // P, P], F32R) for i in range(2)]
        qk_rest = [sb(f"qk_rest{i}", [P, QK // P, P], F32R) for i in range(2)]
        v_out = [sb(f"v_out{i}", [P, E]) for i in range(2)]

        xT_ps = pb("xT_ps", [P, KT, P])
        qk_ps = [pb(f"qk_ps{i}", [P, QKH, D]) for i in range(2)]
        v_ps = pb("v_ps", [P, E])
        qkT_ps = pb("qkT_ps", [P, QK])

        x_loaded = [sem(f"x_loaded{i}") for i in range(2)]
        rope_loaded = [sem(f"rope_loaded{i}") for i in range(2)]
        xstat_done = sem("xstat_done")
        aggregate_open = sem("aggregate_open")
        xstd_done = sem("xstd_done")
        xrstd_done = sem("xrstd_done")
        xn_ready = sem("xn_ready")
        xT_ready = sem("xT_ready")
        hT_ready = sem("hT_ready")
        hT_rounded = sem("hT_rounded")
        hT_split = sem("hT_split")
        qk_summed = sem("qk_summed")
        v_summed = sem("v_summed")
        v_ready = sem("v_ready")
        parts_ready = sem("parts_ready")
        rot_ready = sem("rot_ready")
        hsum_done = sem("hsum_done")
        hmean_ready = sem("hmean_ready")
        cent_ready = sem("cent_ready")
        csq_ready = sem("csq_ready")
        hvar_ready = sem("hvar_ready")
        hstd_ready = sem("hstd_ready")
        hrstd_ready = sem("hrstd_ready")
        qkn_ready = sem("qkn_ready")
        turned = sem("turned")
        qkT_ready = sem("qkT_ready")
        round_ready = sem("round_ready")
        rest_ready = sem("rest_ready")
        round_stored = [sem(f"round_stored{i}") for i in range(2)]
        rest_stored = [sem(f"rest_stored{i}") for i in range(2)]
        w_out_loaded = sem("w_out_loaded")
        first_loaded = sem("first_loaded")
        v_stored = [sem(f"v_stored{i}") for i in range(2)]

        x_v = ins["x"].rearrange("o (t p) e -> (o t) p e", p=P)
        rope_v = ins["rope"].rearrange("(t p) a d -> t p a d", p=P)
        v_dst = v_scr.rearrange("(t p) e -> t p e", p=P)
        qk_dst = qk_scr.rearrange("a (c p) n -> a p c n", p=P)

        FIRST, PEELED, LAST = -2, 6, NB + 2

        def live(t):
            return not isinstance(t, int) or 0 <= t < NB

        def steps(eng, step):
            for s in range(FIRST, PEELED):
                step(s, s % 2)
            with eng.Fori(0, (NB - 2 - PEELED) // 2) as i:
                for b in range(2):
                    step(i * 2 + (PEELED + b), b)
            for s in range(NB - 2, LAST + 1):
                step(s, s % 2)

        def wait(eng, s, value):
            if not isinstance(value, int) or value > 0:
                eng.wait_ge(s, value)

        def dmas(t, par):
            return (t - par) * 8

        block = ctx.enter_context(nc.Block())

        @block.sync
        def _(sp):
            def load_ahead():
                sp.dma_start(keep["w_out"][:, :].rearrange("p (k e) -> p k e", k=KT),
                             ins["w_out"].rearrange("(k p) e -> p k e", p=P)).then_inc(w_out_loaded, 16)
                for par in range(2):
                    sp.wait_ge(round_stored[par], BPC // 2 * 16)
                    sp.wait_ge(rest_stored[par], BPC // 2 * 16)
                for stack, row, parts in ((first_k, E, K_PARTS), (first_q, 0, Q_PARTS)):
                    for a, part in enumerate(parts):
                        src = qk_scr[part, row:row + P, 0:CHUNK].rearrange("(h d) n -> d h n", h=HPG)
                        sp.dma_start(stack[a * D:(a + 1) * D, :, :].bitcast(F32), src).then_inc(first_loaded, 16)

            def step(s, par):
                if isinstance(s, int) and s == NB - 1:
                    load_ahead()
                if live(s + 2):
                    t = s + 2
                    wait(sp, xn_ready, t - 1)
                    sp.dma_start(x_in[par][:, :], x_v[t]).then_inc(x_loaded[par], 16)
                if live(s):
                    wait(sp, parts_ready, s - 1)
                    sp.dma_start(rope[par][:, :, :], rope_v[s]).then_inc(rope_loaded[par], 16)
                if live(s - 1):
                    wait(sp, v_ready, s)
                    sp.dma_start(v_dst[s - 1], v_out[1 - par][:, :]).then_inc(v_stored[1 - par], 16)
                if live(s - 3):
                    t, odd = s - 3, 1 - par
                    wait(sp, round_ready, t + 1)
                    sp.dma_start(qk_dst[0, :, :, bass.ts(t, P)], qk_round[odd][:, :, :].bitcast(F32)).then_inc(round_stored[odd], 16)
                    wait(sp, rest_ready, t + 1)
                    sp.dma_start(qk_dst[1, :, :, bass.ts(t, P)], qk_rest[odd][:, :, :].bitcast(F32)).then_inc(rest_stored[odd], 16)

            steps(sp, step)
            sp.wait_ge(w_out_loaded, 16)
            sp.wait_ge(first_loaded, (len(K_PARTS) + len(Q_PARTS)) * 16)
            for par in range(2):
                sp.wait_ge(v_stored[par], NB // 2 * 16)
                sp.wait_ge(round_stored[par], NB // 2 * 16)
                sp.wait_ge(rest_stored[par], NB // 2 * 16)

        @block.tensor
        def _(pe):
            def step(s, par):
                if live(s + 1):
                    t = s + 1
                    wait(pe, xn_ready, t + 1)
                    wait(pe, hT_ready, t)
                    for k in range(KT):
                        mm = pe.transpose(xT_ps[:, k, :], xn[1 - par][:, k * P:(k + 1) * P], ident[:, :])
                    mm.then_inc(xT_ready, 1)
                if live(s - 3):
                    t = s - 3
                    wait(pe, qkn_ready, t + 1)
                    wait(pe, qkT_ready, t)
                    for c in range(QK // P):
                        mm = pe.transpose(qkT_ps[:, c * P:(c + 1) * P], qkn[:, c * HPG:(c + 1) * HPG, :], ident[:, :])
                    mm.then_inc(turned, 1)
                if live(s):
                    wait(pe, hT_split, s + 1)
                    wait(pe, parts_ready, s - 1)
                    for c, dst in enumerate((qk_ps[par][:, 0:H, :], qk_ps[par][:, H:2 * H, :], v_ps[:, :])):
                        if c == 2:
                            wait(pe, v_ready, s)
                        for k in range(KT):
                            for n, (hp, wp) in enumerate(PRODUCTS):
                                mm = pe.matmul(dst, hT_parts[par][hp][:, k, :], w_parts[wp][:, k, c * E:(c + 1) * E],
                                               start=(k == 0 and n == 0), stop=(k == KT - 1 and n == 2))
                        if c == 1:
                            mm.then_inc(qk_summed, 1)
                        elif c == 2:
                            mm.then_inc(v_summed, 1)

            steps(pe, step)

        @block.vector
        def _(dve):
            def step(s, par):
                odd = 1 - par
                if live(s - 1):
                    t = s - 1
                    wait(dve, qk_summed, t + 1)
                    wait(dve, rope_loaded[odd], dmas(t, odd) + 16)
                    wait(dve, rot_ready, t)
                    table = rope[odd]
                    dve.tensor_tensor(rot_cos[:, :, :], qk_ps[odd][:, :, :],
                                      table[:, 0:1, :].broadcast_to([P, QKH, D]), ALU.mult)
                    dve.tensor_tensor(rot_sin[:, :, 0:HALF], qk_ps[odd][:, :, HALF:D],
                                      table[:, 1:2, 0:HALF].broadcast_to([P, QKH, HALF]), ALU.mult)
                    dve.tensor_tensor(rot_sin[:, :, HALF:D], qk_ps[odd][:, :, 0:HALF],
                                      table[:, 1:2, HALF:D].broadcast_to([P, QKH, HALF]), ALU.mult).then_inc(parts_ready, 1)
                if live(s + 1):
                    t = s + 1
                    wait(dve, hT_ready, t + 1)
                    wait(dve, v_summed, t - 1)
                    dve.tensor_copy(hT_parts[odd][0][:, :, :], hT[:, :, :]).then_inc(hT_rounded, 1)
                if live(s - 2):
                    t = s - 2
                    wait(dve, csq_ready, t + 1)
                    dve.tensor_reduce(hvar[:, :], csq[:, :, :], AX.X, ALU.add).then_inc(hvar_ready, 1)
                if live(s + 2):
                    t = s + 2
                    wait(dve, x_loaded[par], dmas(t, par) + 16)
                    wait(dve, xrstd_done, t)
                    dve.bn_stats(x_stats[:, :], x_in[par][:, :]).then_inc(xstat_done, 1)
                    wait(dve, xstat_done, t * 2 + 1)
                if live(s - 3):
                    t = s - 3
                    wait(dve, qkT_ready, t + 1)
                    wait(dve, round_stored[odd], dmas(t, odd))
                    dve.tensor_copy(qk_round[odd][:, :, :].rearrange("p c n -> p (c n)"), qkT[:, :]).then_inc(round_ready, 1)
                if live(s + 2):
                    wait(dve, xn_ready, s + 2)
                    dve.sem_inc(aggregate_open, 1)
                    dve.bn_aggr(x_mv[:, :], x_stats[:, :]).then_inc(xstat_done, 1)
                if live(s - 2):
                    t = s - 2
                    wait(dve, hstd_ready, t + 1)
                    dve.reciprocal(hrstd[:, :], hstd[:, :]).then_inc(hrstd_ready, 1)
                if live(s + 2):
                    t = s + 2
                    wait(dve, xstd_done, t + 1)
                    dve.reciprocal(x_rstd[:, :], x_std[:, :]).then_inc(xrstd_done, 1)
                if live(s - 2):
                    t = s - 2
                    wait(dve, hrstd_ready, t + 1)
                    wait(dve, turned, t)
                    dve.tensor_tensor(qkn[:, :, :], cent[par][:, :, :],
                                      hrstd[:, :].unsqueeze(2).broadcast_to([P, QKH, D]), ALU.mult).then_inc(qkn_ready, 1)
                if live(s + 2):
                    t = s + 2
                    wait(dve, xrstd_done, t + 1)
                    wait(dve, xT_ready, t - 1)
                    dve.tensor_scalar(xn[par][:, :], x_in[par][:, :], x_mv[:, 0:1], x_rstd[:, :],
                                      ALU.subtract, ALU.mult).then_inc(xn_ready, 1)
                if live(s - 1):
                    t = s - 1
                    wait(dve, rot_ready, t + 1)
                    dve.tensor_reduce(hsum[:, :], rot[:, :, :], AX.X, ALU.add).then_inc(hsum_done, 1)
                    wait(dve, hsum_done, t + 1)
                    wait(dve, cent_ready, t)
                    dve.tensor_scalar(hmean[:, :], hsum[:, :], 1.0 / D, None, ALU.mult).then_inc(hmean_ready, 1)

            steps(dve, step)

        @block.scalar
        def _(act):
            def step(s, par):
                odd = 1 - par
                if live(s + 1):
                    t = s + 1
                    wait(act, xT_ready, t + 1)
                    wait(act, hT_split, t)
                    for k in range(KT):
                        op = act.activation(hT[:, k, :], xT_ps[:, k, :], ACT.Identity, bias=cols[:, 0, k:k + 1],
                                            scale=cols[:, 1, k:k + 1])
                    op.then_inc(hT_ready, 1)
                if live(s - 2):
                    t = s - 2
                    wait(act, cent_ready, t + 1)
                    wait(act, hvar_ready, t)
                    act.activation(csq[:, :, :], cent[par][:, :, :], ACT.Square).then_inc(csq_ready, 1)
                if live(s - 3):
                    t = s - 3
                    wait(act, turned, t + 1)
                    wait(act, round_ready, t)
                    wait(act, rest_ready, t)
                    act.activation(qkT[:, :], qkT_ps[:, :], ACT.Identity, bias=keep["qk_bias"][:, :],
                                   scale=keep["qk_scale"][:, :]).then_inc(qkT_ready, 1)
                if live(s - 1):
                    t = s - 1
                    wait(act, v_summed, t + 1)
                    wait(act, v_stored[odd], dmas(t, odd))
                    act.activation(v_out[odd][:, :], v_ps[:, :], ACT.Copy).then_inc(v_ready, 1)
                if live(s - 2):
                    t = s - 2
                    wait(act, hvar_ready, t + 1)
                    act.activation(hstd[:, :], hvar[:, :], ACT.Sqrt, bias=eps[:, :], scale=1.0 / D).then_inc(hstd_ready, 1)
                if live(s + 2):
                    t = s + 2
                    wait(act, xstat_done, t * 2 + 2)
                    act.activation(x_std[:, :], x_mv[:, 1:2], ACT.Sqrt, bias=eps[:, :]).then_inc(xstd_done, 1)

            steps(act, step)

        @block.gpsimd
        def _(pool):
            def step(s, par):
                odd = 1 - par
                if live(s - 1):
                    t = s - 1
                    wait(pool, parts_ready, t + 1)
                    wait(pool, hsum_done, t)
                    wait(pool, cent_ready, t)
                    pool.tensor_tensor(rot[:, :, :], rot_cos[:, :, :], rot_sin[:, :, :], ALU.add).then_inc(rot_ready, 1)
                if live(s + 1):
                    t = s + 1
                    wait(pool, hT_rounded, t + 1)
                    wait(pool, v_summed, t - 1)
                    pool.tensor_tensor(hT_parts[odd][1][:, :, :], hT[:, :, :], hT_parts[odd][0][:, :, :].bitcast(F32),
                                       ALU.subtract).then_inc(hT_split, 1)
                if live(s - 3):
                    t = s - 3
                    wait(pool, round_ready, t + 1)
                    wait(pool, rest_stored[odd], dmas(t, odd))
                    pool.tensor_tensor(qk_rest[odd][:, :, :].rearrange("p c n -> p (c n)"), qkT[:, :],
                                       qk_round[odd][:, :, :].rearrange("p c n -> p (c n)").bitcast(F32),
                                       ALU.subtract).then_inc(rest_ready, 1)
                if live(s - 1):
                    t = s - 1
                    wait(pool, hmean_ready, t + 1)
                    wait(pool, qkn_ready, t - 1)
                    wait(pool, csq_ready, t - 1)
                    pool.tensor_tensor(cent[odd][:, :, :], rot[:, :, :],
                                       hmean[:, :].unsqueeze(2).broadcast_to([P, QKH, D]), ALU.subtract).then_inc(cent_ready, 1)

            steps(pool, step)


def attention_phase(nc, keep, first_k, first_q, ins, qk_scr, v_scr, att_scr):
    with ExitStack() as ctx:
        sb = lambda name, shape, dt=F32: ctx.enter_context(nc.sbuf_tensor(name, shape, dt))
        sem = lambda name: ctx.enter_context(nc.semaphore(name))
        QBUF, SQBUF, POWBUF, SUMBUF, LAG = 2, 4, 12, 4, 5
        SCOREBUF = 3
        WEIGH_LAG = 2
        SUM_LAG = 2
        PAIR = 2
        HALVES = HPG // PAIR
        PIECES = 4
        PIECE = CHUNK // PIECES
        APART = 3

        k_stack = [first_k] + [sb(f"k_stack{c}", [P, HPG, CHUNK], F32R) for c in range(1, NCH)]
        v_grp = sb("v_grp", [P, NB, P])
        q_stack = [first_q] + [sb(f"q_stack{i}", [P, HPG, CHUNK], F32R) for i in range(1, QBUF)]
        squares = [sb(f"squares{i}", [P, PAIR, CHUNK]) for i in range(SQBUF)]
        powers = [sb(f"powers{i}", [P, PAIR, CHUNK]) for i in range(POWBUF)]
        sums = [sb(f"sums{i}", [P, PAIR, CHUNK]) for i in range(SUMBUF)]
        ones = sb("ones", [P, D])
        inv_den = sb("inv_den", [P, CHUNK])
        att = [sb(f"att{i}", [P, CHUNK]) for i in range(2)]
        weights = keep["feed"][:, :].rearrange("p (k e) -> p k e", k=KT)
        first_att = keep["feed"][:, :].rearrange("p (g n) -> p g n", g=NG)
        piece_max = sb("piece_max", [P, 3, NG * PIECES])
        own_max = sb("own_max", [P, 6])
        num = sb("num", [P, CHUNK])
        den = sb("den", [P, CHUNK])
        score_ps = [ctx.enter_context(nc.psum_tensor(f"score_ps{i}", [P, PAIR, CHUNK], F32)) for i in range(SCOREBUF)]
        num_ps = ctx.enter_context(nc.psum_tensor("num_ps", [P, CHUNK], F32))
        den_ps = ctx.enter_context(nc.psum_tensor("den_ps", [P, CHUNK], F32))

        k_loaded = [sem(f"k_loaded{c}") for c in range(NCH)]
        v_loaded = [sem(f"v_loaded{c}") for c in range(NCH)]
        q_loaded = [sem(f"q_loaded{i}") for i in range(QBUF)]
        kv_free = sem("kv_free")
        q_free = sem("q_free")
        ones_ready = sem("ones_ready")
        scores_ready = sem("scores_ready")
        squares_ready = sem("squares_ready")
        masked_ready = sem("masked_ready")
        select_open = sem("select_open")
        dma_open = sem("dma_open")
        load_open = sem("load_open")
        dve_powers = sem("dve_powers")
        act_powers = sem("act_powers")
        step_used = sem("step_used")
        sums_ready = sem("sums_ready")
        sums_used = sem("sums_used")
        inverse_ready = sem("inverse_ready")
        totals_taken = sem("totals_taken")
        att_ready = sem("att_ready")
        att_stored = [sem(f"att_stored{i}") for i in range(2)]
        weights_loaded = sem("weights_loaded")
        surveyed = sem("surveyed")
        own_ready = sem("own_ready")
        sizes_ready = sem("sizes_ready")
        first_att_loaded = sem("first_att_loaded")

        steps = [(j, i) for j in range(NCH) for i in range(BPC * (j + 1))]
        S = len(steps)
        U = HALVES * S
        diagonals = [u for u in range(U) if steps[u // HALVES][1] >= BPC * steps[u // HALVES][0]]
        chunk_end = [max(st for st in range(S) if steps[st][0] == j) for j in range(NCH)]
        last_use = {max(st for st in range(S) if steps[st][1] == BPC * c + BPC - 1): c for c in range(NCH)}
        pair_starts = [st for st, (j, i) in enumerate(steps) if i < BPC * j and i % 2 == 0 and (2 * j - 1 - i // 2) % 4 != 0]
        adds = [(st, half) for st in pair_starts for half in range(HALVES)]
        summed = {HALVES * (st + second) + half: n for n, (st, half) in enumerate(adds) for second in range(2)}
        by_act = [u for u in range(U) if u not in diagonals and u % 8 == 7]
        by_dve = [u for u in range(U) if u not in by_act]
        AP, DP, A = len(by_act), len(by_dve), len(adds)

        def den_items(s):
            direct = [("powers", s - WEIGH_LAG)] if s >= WEIGH_LAG and HALVES * (s - WEIGH_LAG) not in summed else []
            return direct + [("sum", st) for st in pair_starts if st + 1 + WEIGH_LAG + SUM_LAG == s]

        den_order = [[item for s in range(S + WEIGH_LAG) for item in den_items(s) if steps[item[1]][0] == j] for j in range(NCH)]

        def first_query(u):
            j, i = steps[u // HALVES]
            return max(0, i - BPC * j) * P

        def up_to(members, u):
            return sum(m <= u for m in members)

        def wait(eng, s, value):
            if not isinstance(value, int) or value > 0:
                eng.wait_ge(s, value)

        def wait_powers(eng, g, u):
            if u in by_act:
                wait(eng, act_powers, g * AP + up_to(by_act, u))
            else:
                wait(eng, dve_powers, g * DP + (up_to(by_dve, u) if u >= 0 else u + 1))

        def wait_powers_free(eng, g, u):
            wait(eng, step_used, g * S + (u - POWBUF + HALVES) // HALVES)
            if u - POWBUF in summed:
                wait(eng, sums_ready, g * A + (summed[u - POWBUF] + 1))

        def groups(eng, group):
            group(0)
            with eng.Fori(1, NG) as g:
                group(g)

        def is_first(g):
            return isinstance(g, int) and g == 0

        k_src = qk_scr[:, E:2 * E, :].rearrange("a (g h d) n -> a g d h n", g=NG, h=HPG)
        q_src = qk_scr[:, 0:E, :].rearrange("a (g h d) n -> a g d h n", g=NG, h=HPG)
        v_src = v_scr.rearrange("(t p) (g e) -> g p t e", p=P, g=NG)
        att_dst = att_scr.rearrange("(g p) n -> g p n", g=NG)
        quarters = [ins[w].rearrange("(k p) (g n) -> g p k n", p=P, g=NG) for w in ("w_gate", "w_up")]
        quarters.append(ins["w_down"].rearrange("(g k p) n -> g p k n", p=P, g=NG))
        SURVEY_AT = (104, 144, 192)
        w_out = keep["w_out"][:, :].rearrange("p (k e) -> p k e", k=KT)
        block = ctx.enter_context(nc.Block())

        @block.sync
        def _(sp):
            def group(g):
                for c in range(NCH):
                    wait(sp, kv_free, g * NCH + (c + 1 - NCH))
                    sp.sem_inc(load_open, 1)
                    there = is_first(g) and c == 0
                    for a, part in enumerate(K_PARTS):
                        if not there:
                            sp.dma_start(k_stack[c][a * D:(a + 1) * D, :, :].bitcast(F32),
                                         k_src[part, g, :, :, c * CHUNK:(c + 1) * CHUNK]).then_inc(k_loaded[c], 16)
                    wait(sp, q_free, g * NCH + (c + 1 - QBUF))
                    sp.sem_inc(load_open, 1)
                    for a, part in enumerate(Q_PARTS):
                        if not there:
                            sp.dma_start(q_stack[c % QBUF][a * D:(a + 1) * D, :, :].bitcast(F32),
                                         q_src[part, g, :, :, c * CHUNK:(c + 1) * CHUNK]).then_inc(q_loaded[c % QBUF], 16)
                    sp.dma_start(v_grp[:, c * BPC:(c + 1) * BPC, :],
                                 v_src[g, :, c * BPC:(c + 1) * BPC, :]).then_inc(v_loaded[c], 16)

            groups(sp, group)
            sp.wait_ge(att_stored[0], ((NG - 1) * (NCH // 2) + 1) * 16)
            sp.wait_ge(surveyed, 3 * PIECES * NG)
            sp.dma_start(first_att, att_scr.rearrange("(g p) n -> p g n", p=P)[:, :, 0:CHUNK]).then_inc(first_att_loaded, 16)
            sp.wait_ge(first_att_loaded, 16)

        @block.tensor
        def _(pe):
            pe.wait_ge(ones_ready, 1)

            def scores(g, u):
                st, half = u // HALVES, u % HALVES
                j, i = steps[st]
                n0 = first_query(u)
                if i == 0 and half == 0:
                    before = 1 if j % QBUF == 0 else 0
                    wait(pe, q_loaded[j % QBUF], (g * (NCH // QBUF) + (j // QBUF + 1 - before)) * (16 * len(Q_PARTS)))
                if i == BPC * j and half == 0:
                    wait(pe, k_loaded[j], (g + (1 if j > 0 else 0)) * (16 * len(K_PARTS)))
                wait(pe, squares_ready, g * U + (u - SCOREBUF + 1))
                for h in range(PAIR):
                    hh = half * PAIR + h
                    mm = pe.matmul(score_ps[u % SCOREBUF][:, h, n0:], k_stack[i // BPC][:, hh, i % BPC * P:(i % BPC + 1) * P],
                                   q_stack[j % QBUF][:, hh, n0:], start=True, stop=True)
                    before = st - WEIGH_LAG - 1
                    if half == 0 and h == 0 and (before in last_use or before + S in last_use and not is_first(g)):
                        mm.then_inc(kv_free, 1)
                mm.then_inc(scores_ready, 1)

            def numerators(g, st):
                j, i = steps[st]
                n0 = first_query(HALVES * st)
                if i == 0:
                    wait(pe, totals_taken, g * NCH + j)
                if i == BPC * j:
                    pe.wait_ge(v_loaded[j], (g + 1) * 16)
                for half in range(HALVES):
                    u = HALVES * st + half
                    wait_powers(pe, g, u)
                    for h in range(PAIR):
                        hh = half * PAIR + h
                        mm = pe.matmul(num_ps[hh * D:(hh + 1) * D, n0:], v_grp[:, i, hh * D:(hh + 1) * D],
                                       powers[u % POWBUF][:, h, n0:], start=(i == 0), stop=(st == chunk_end[j]))
                        if hh == 0 and st in chunk_end:
                            mm.then_inc(q_free, 1)
                if HALVES * st in summed:
                    mm.then_inc(step_used, 1)

            def denominators(g, item):
                kind, st = item
                j = steps[st][0]
                n0 = first_query(HALVES * st)
                for hh in range(HPG):
                    half, h = hh // PAIR, hh % PAIR
                    if kind == "powers":
                        src = powers[(HALVES * st + half) % POWBUF]
                    else:
                        n = adds.index((st, half))
                        src = sums[n % SUMBUF]
                        if h == 0:
                            pe.wait_ge(sums_ready, g * A + (n + 1))
                    mm = pe.matmul(den_ps[hh * D:(hh + 1) * D, n0:], ones[:, :], src[:, h, n0:],
                                   start=(item == den_order[j][0]), stop=(item == den_order[j][-1]))
                    if kind == "sum" and h == PAIR - 1:
                        mm.then_inc(sums_used, 1)
                if kind == "powers":
                    mm.then_inc(step_used, 1)

            def group(g):
                for s in range(S):
                    of, turn = (g, s) if s >= WEIGH_LAG else (g - 1, s + S)
                    begun = s >= WEIGH_LAG or not is_first(g)
                    scores(g, HALVES * s)
                    scores(g, HALVES * s + 1)
                    if begun:
                        numerators(of, turn - WEIGH_LAG)
                        for item in den_items(turn):
                            denominators(of, item)

            groups(pe, group)
            for turn in range(S, S + WEIGH_LAG):
                numerators(NG - 1, turn - WEIGH_LAG)
                for item in den_items(turn):
                    denominators(NG - 1, item)

        @block.scalar
        def _(act):
            def take_totals(g, j):
                wait(act, step_used, g * S + (chunk_end[j] + 1))
                wait(act, att_ready, g * NCH + j)
                act.activation(num[:, :], num_ps[:, :], ACT.Copy)
                act.activation(den[:, :], den_ps[:, :], ACT.Copy).then_inc(totals_taken, 1)

            def group(g):
                for u in range(U):
                    n0 = first_query(u)
                    act.wait_ge(scores_ready, g * U + (u + 1))
                    wait_powers(act, g, u - SQBUF)
                    act.activation(squares[u % SQBUF][:, :, n0:], score_ps[u % SCOREBUF][:, :, n0:], ACT.Square).then_inc(squares_ready, 1)
                    if u - 1 in by_act:
                        m = u - 1
                        act.wait_ge(squares_ready, g * U + (m + 1))
                        wait_powers_free(act, g, m)
                        act.activation(powers[m % POWBUF][:, :, :], squares[m % SQBUF][:, :, :], ACT.Square).then_inc(act_powers, 1)
                    for j in range(NCH):
                        at = HALVES * (chunk_end[j] + 1 + WEIGH_LAG) - 1
                        if u == at:
                            take_totals(g, j)
                        if u == at - U and not is_first(g):
                            take_totals(g - 1, j)

            groups(act, group)
            take_totals(NG - 1, NCH - 1)

        @block.gpsimd
        def _(pool):
            def select(g, u):
                n0 = first_query(u)
                pool.wait_ge(squares_ready, g * U + (u + 1))
                pool.sem_inc(select_open, 1)
                corner = squares[u % SQBUF][:, :, n0:n0 + P]
                pool.affine_select(out=corner, in_=corner, compare_op=ALU.is_ge, fill=0.0, base=0,
                                   pattern=[[0, PAIR], [1, P]], channel_multiplier=-1).then_inc(masked_ready, 1)

            def add(g, n):
                st, half = adds[n]
                u = HALVES * st + half
                wait(pool, sums_used, g * A + (n - SUMBUF + 1))
                wait_powers(pool, g, u)
                wait_powers(pool, g, u + HALVES)
                pool.tensor_tensor(sums[n % SUMBUF][:, :, :], powers[u % POWBUF][:, :, :],
                                   powers[(u + HALVES) % POWBUF][:, :, :], ALU.add).then_inc(sums_ready, 1)

            def store(g, j):
                pool.wait_ge(att_ready, g * NCH + (j + 1))
                pool.sem_inc(dma_open, 1)
                pool.dma_start(att_dst[g, :, j * CHUNK:(j + 1) * CHUNK], att[j % 2][:, :]).then_inc(att_stored[j % 2], 16)

            def store_before(g, j):
                if not is_first(g):
                    store(g - 1, j)

            def load_weights(g, t):
                wait(pool, surveyed, (g * 3 + t) * PIECES)
                pool.sem_inc(dma_open, 1)
                pool.dma_start(weights[:, :, :], quarters[t][g]).then_inc(weights_loaded, 16)

            events = [(u, select, u) for u in diagonals]
            events += [(HALVES * (adds[n][0] + 1) + adds[n][1] + 0.5, add, n) for n in range(A)]
            stores = [HALVES * chunk_end[j] + LAG + APART * PIECES + 4.5 for j in range(NCH)]
            events += [(at, store, j) if at < U else (at - U, store_before, j) for j, at in enumerate(stores)]
            events += [(at - 20.5, load_weights, t) for t, at in enumerate(SURVEY_AT)]
            events.sort(key=lambda event: event[0])

            def group(g):
                for _, stage, n in events:
                    stage(g, n)

            groups(pool, group)
            store(NG - 1, NCH - 1)
            pool.wait_ge(own_ready, 6)
            pool.partition_all_reduce(keep["sizes"][:, :], own_max[:, :], channels=P, reduce_op=RMAX).then_inc(sizes_ready, 1)
            for i in range(2):
                pool.wait_ge(att_stored[i], NG * NCH // 2 * 16)

        @block.vector
        def _(dve):
            dve.memset(ones[:, :], 1.0).then_inc(ones_ready, 1)
            for k in range(KT):
                dve.tensor_tensor(w_out[:, k, :], w_out[:, k, :], keep["gate_a"][:, :], ALU.mult)

            def normalise(g, j, p):
                part = slice(p * PIECE, (p + 1) * PIECE)
                dve.wait_ge(totals_taken, g * NCH + (j + 1))
                if p == 0:
                    wait(dve, att_ready, g * NCH + j)
                dve.reciprocal(inv_den[:, part], den[:, part]).then_inc(inverse_ready, 1)
                if p == PIECES - 1:
                    wait(dve, att_stored[j % 2], (g * (NCH // 2) + j // 2) * 16)
                    dve.wait_ge(inverse_ready, (g * NCH + (j + 1)) * PIECES)
                    dve.tensor_tensor(att[j % 2][:, :], num[:, :], inv_den[:, :], ALU.mult).then_inc(att_ready, 1)

            def survey(g, t, p):
                dve.wait_ge(weights_loaded, (g * 3 + (t + 1)) * 16)
                dve.tensor_reduce(piece_max[:, t, bass.ts(g * PIECES + p, 1)], weights[:, p, :], axis=AX.X, op=ALU.max,
                                  apply_absolute_value=True).then_inc(surveyed, 1)

            def group(g):
                for u in range(U):
                    n0 = first_query(u)
                    if u in by_dve:
                        if u in diagonals:
                            dve.wait_ge(masked_ready, g * len(diagonals) + (diagonals.index(u) + 1))
                        else:
                            dve.wait_ge(squares_ready, g * U + (u + 1))
                        wait_powers_free(dve, g, u)
                        sq = squares[u % SQBUF][:, :, n0:]
                        dve.tensor_tensor(powers[u % POWBUF][:, :, n0:], sq, sq, ALU.mult).then_inc(dve_powers, 1)
                    for j in range(NCH):
                        after = u - (HALVES * chunk_end[j] + HALVES + LAG)
                        if after % APART == 0 and 0 <= after // APART < PIECES:
                            normalise(g, j, after // APART)
                        if 0 <= after + U < PIECES and not is_first(g):
                            normalise(g - 1, j, after + U)
                    for t, at in enumerate(SURVEY_AT):
                        if (u - at) % APART == 0 and 0 <= (u - at) // APART < PIECES:
                            survey(g, t, (u - at) // APART)

            groups(dve, group)
            for p in range(PIECES):
                normalise(NG - 1, NCH - 1, p)
            dve.wait_ge(surveyed, 3 * PIECES * NG)
            for t in range(3):
                dve.tensor_reduce(own_max[:, t:t + 1], piece_max[:, t, :], axis=AX.X, op=ALU.max).then_inc(own_ready, 1)
            for t, src in ((3, keep["cols"][:, 3, :]), (4, keep["cols"][:, 2, :]), (5, keep["gate_b"][:, :])):
                dve.tensor_reduce(own_max[:, t:t + 1], src, axis=AX.X, op=ALU.max, apply_absolute_value=True).then_inc(own_ready, 1)


def mlp_phase(nc, keep, ins, att_scr, out):
    with ExitStack() as ctx:
        sb = lambda name, shape, dt=F32: ctx.enter_context(nc.sbuf_tensor(name, shape, dt))
        sem = lambda name: ctx.enter_context(nc.semaphore(name))
        ident, cols, eps, sizes = keep["ident"], keep["cols"], keep["eps"], keep["sizes"]
        PL = 4
        IC = INNER // (PL * P)
        KI = INNER // P
        PARTS = 2
        HALF = KT // 2
        FIRST_BANKS = (2, 3)
        LAST_BANKS = (0, 1)
        BANKS = FIRST_BANKS + LAST_BANKS
        PRODUCTS = ((0, 0), (0, 1), (1, 0))
        PPC = IC * PL
        TINY = 2.0 ** -30
        EXPONENT = 0x7F800000

        w_out = keep["w_out"][:, :].rearrange("p (k e) -> p k e", k=KT)
        w_gate = sb("w_gate", [P, PARTS, KT, IC, PL, P], F16)
        w_up = sb("w_up", [P, PARTS, KT, IC, PL, P], F16)
        w_down = sb("w_down", [P, PARTS, KI, E], F16)
        staged = [sb(f"staged{i}", [P, HALF, PL * P]) for i in range(2)]
        feed = keep["feed"]
        att = feed[:, :].rearrange("p (g n) -> p g n", g=NG)
        xn = feed[:, :].rearrange("p (b e) -> p b e", b=BPC)
        x_mid = [sb(f"x_mid{i}", [P, BPC, E]) for i in range(2)]
        stats = sb("stats", [P, BPC, 6])
        mv = sb("mv", [P, BPC, 2])
        std = sb("std", [P, BPC])
        rstd = sb("rstd", [P, BPC])
        turned = sb("turned", [P, CHUNK])
        hT = [sb(f"hT_mid{i}", [P, PARTS, KT, CHUNK], F16) for i in range(2)]
        silu = [sb(f"silu{i}", [P, CHUNK]) for i in range(2)]
        hid = [sb(f"hid{i}", [P, PL, CHUNK]) for i in range(2)]
        size = sb("size", [P, PL, CHUNK])
        early = sb("early", [P, 3, CHUNK], BF16)
        late = sb("late", [P, 3, CHUNK], BF16)
        score = sb("score", [P, PL, CHUNK], BF16)
        kept = sb("kept", [P, PARTS, PL, CHUNK], F16)
        bound = sb("bound", [P, 4])
        power = sb("power", [P, 4])
        inverse = sb("inverse", [P, 4])
        scale = sb("scale", [P, 4])
        root = sb("root", [P, 2])
        kept_scale = sb("kept_scale", [P, 1])
        unscale = sb("unscale", [P, 3])
        shift_b = sb("shift_b", [P, KT])
        scale_b = sb("scale_b", [P, KT])
        ring = [ctx.enter_context(nc.psum_tensor(f"ring{i}", [P, E], F32)) for i in range(4)]
        y_ps = [ctx.enter_context(nc.psum_tensor(f"y_ps{i}", [P, E], F32)) for i in range(BPC)]

        staged_loaded = [sem(f"staged_loaded{i}") for i in range(2)]
        down_gated = sem("down_gated")
        w_high = sem("w_high")
        w_rest = sem("w_rest")
        scale_step = sem("scale_step")
        att_loaded = sem("att_loaded")
        x_loaded = [sem(f"xr_loaded{i}") for i in range(2)]
        projected = sem("projected")
        mid_ready = sem("mid_ready")
        stat_step = sem("stat_step")
        norm_open = sem("norm_open")
        std_ready = sem("std_ready")
        rstd_ready = sem("rstd_ready")
        xn_ready = sem("xnm_ready")
        xT_ready = sem("xTm_ready")
        turned_ready = sem("turned_ready")
        high_ready = sem("high_ready")
        hT_ready = sem("hTm_ready")
        pair_ready = sem("pair_ready")
        silu_ready = sem("silu_ready")
        hid_ready = sem("hid_ready")
        size_ready = sem("size_ready")
        early_ready = sem("early_ready")
        late_ready = sem("late_ready")
        part_ready = sem("part_ready")
        score_ready = sem("score_ready")
        select_ready = sem("select_ready")
        kept_high = sem("kept_high")
        kept_ready = sem("kept_ready")
        down_done = sem("down_done")
        y_ready = sem("y_ready")
        out_ready = sem("out_ready")
        out_stored = [sem(f"out_stored{i}") for i in range(2)]

        x_v = ins["x"].rearrange("o (c b p) e -> (o c) p b e", p=P, b=BPC)
        out_v = out.rearrange("o (c b p) e -> (o c) p b e", p=P, b=BPC)
        att_v = att_scr.rearrange("(g p) (c n) -> c p g n", p=P, n=CHUNK)
        gate_v = ins["w_gate"].rearrange("(k p) (i n) -> i p k n", p=P, i=IC)
        up_v = ins["w_up"].rearrange("(k p) (i n) -> i p k n", p=P, i=IC)
        down_v = ins["w_down"].rearrange("(i p a) e -> i p a e", p=P, a=PL)
        FIRST_STAGES = [(kind, 0, h) for kind in ("gate", "up") for h in range(2)]
        SLICE_STAGES = [[(kind, i + 1, h) for kind in ("gate", "up") for h in range(2) if i + 1 < IC] +
                        [("down", i, h) for h in range(2)] for i in range(IC)]
        STAGES = FIRST_STAGES + [stage for stages in SLICE_STAGES for stage in stages]
        BEFORE = 2
        SRC = {"gate": gate_v, "up": up_v, "down": down_v}

        def parts_up_to(kind, i):
            return STAGES.index((kind, i, 1)) + 1

        def staged_with(i, a):
            return [STAGES.index(stage) for stage in SLICE_STAGES[i][2 * a:2 * a + 2]]

        def chunks(eng, chunk):
            chunk(0, 0)
            with eng.Fori(0, (NCH - 2) // 2) as i:
                for b in range(2):
                    chunk(i * 2 + (1 + b), 1 - b)
            chunk(NCH - 1, (NCH - 1) % 2)

        def last(c):
            return isinstance(c, int) and c == NCH - 1

        def wait(eng, s, value):
            if not isinstance(value, int) or value > 0:
                eng.wait_ge(s, value)

        def dmas(c, par):
            return (c - par) * 8

        block = ctx.enter_context(nc.Block())

        @block.sync
        def _(sp):
            def load(c, par):
                if not (isinstance(c, int) and c == 0):
                    wait(sp, xT_ready, c * KT)
                    sp.dma_start(att, att_v[c]).then_inc(att_loaded, 16)
                wait(sp, out_stored[par], dmas(c, par))
                sp.dma_start(x_mid[par][:, :, :], x_v[c]).then_inc(x_loaded[par], 16)

            load(0, 0)

            def chunk(c, par):
                if not (isinstance(c, int) and c == 0):
                    wait(sp, out_ready, c * BPC)
                    sp.dma_start(out_v[c - 1], x_mid[1 - par][:, :, :]).then_inc(out_stored[1 - par], 16)
                if not last(c):
                    load(c + 1, 1 - par)

            chunks(sp, chunk)
            sp.wait_ge(out_ready, NCH * BPC)
            sp.dma_start(out_v[NCH - 1], x_mid[(NCH - 1) % 2][:, :, :]).then_inc(out_stored[(NCH - 1) % 2], 16)
            for par in range(2):
                sp.wait_ge(out_stored[par], NCH // 2 * 16)

        @block.gpsimd
        def _(pool):
            for n, (kind, i, h) in enumerate(STAGES):
                if n >= 2:
                    pool.wait_ge(w_high, n - 1)
                    pool.wait_ge(w_rest, n - 1)
                pool.dma_start(staged[n % 2][:, :, :], SRC[kind][i][:, h * HALF:(h + 1) * HALF, :]).then_inc(staged_loaded[n % 2], 16)

        @block.tensor
        def _(pe):
            def project(c, banks):
                wait(pe, att_loaded, c * 16)
                for b in banks:
                    if b == banks[0]:
                        wait(pe, hid_ready, (c - 1) * PPC + (2 * PL + 2 if banks == FIRST_BANKS else 2 * PL + 3))
                    for k in range(NG):
                        mm = pe.matmul(ring[b][:, :], att[:, k, b * P:(b + 1) * P], w_out[:, k, :],
                                       start=(k == 0), stop=(k == NG - 1))
                    mm.then_inc(projected, 1)

            def turn(c, banks):
                wait(pe, xn_ready, c * BPC + BPC)
                for k in banks:
                    if k == banks[0]:
                        wait(pe, hid_ready, (c - 1) * PPC + (3 * PL + 2 if banks == FIRST_BANKS else 3 * PL + 3))
                    for b in range(BPC):
                        mm = pe.transpose(ring[k][:, b * P:(b + 1) * P], xn[:, b, k * P:(k + 1) * P], ident[:, :])
                    mm.then_inc(xT_ready, 1)

            def gate_up(c, par, n):
                i, a = n // PL, n % PL
                if isinstance(c, int) and c == 0 and a == 0:
                    pe.wait_ge(w_rest, parts_up_to("up", i))
                    pe.wait_ge(w_high, parts_up_to("up", i))
                if n == 0:
                    wait(pe, hT_ready, (c + 1) * KT)
                if n in (2 * PL + 3, 2 * PL + 4) and not last(c):
                    wait(pe, mid_ready, (c + 1) * BPC + 2 * (n - 2 * PL - 2))
                elif n == 3 * PL + 3 and not last(c):
                    wait(pe, turned_ready, (c + 1) * KT + 2)
                else:
                    wait(pe, hid_ready, c * PPC + (n - 1))
                for w, bank in ((w_gate, ring[2 * (n % 2)]), (w_up, ring[2 * (n % 2) + 1])):
                    for k in range(KT):
                        for m, (wp, hp) in enumerate(PRODUCTS):
                            mm = pe.matmul(bank[:, :], w[:, wp, k, i, a, :], hT[par][:, hp, k, :],
                                           start=(k == 0 and m == 0), stop=(k == KT - 1 and m == 2))
                mm.then_inc(pair_ready, 1)

            def down(c, i):
                if isinstance(c, int) and c == 0:
                    pe.wait_ge(w_rest, parts_up_to("down", i))
                    pe.wait_ge(w_high, parts_up_to("down", i))
                wait(pe, kept_ready, c * IC + (i + 1))
                if i == 0:
                    wait(pe, out_ready, c * BPC)
                for b in range(BPC):
                    for a in range(PL):
                        for m, (kp, wp) in enumerate(PRODUCTS):
                            mm = pe.matmul(y_ps[b][:, :], kept[:, kp, a, b * P:(b + 1) * P],
                                           w_down[:, wp, i * PL + a, :], start=(i == 0 and a == 0 and m == 0),
                                           stop=(i == IC - 1 and a == PL - 1 and m == 2))
                    if b < BPC - 1:
                        if i == IC - 1:
                            mm.then_inc(y_ready, 1)
                    elif i < IC - 1:
                        mm.then_inc(down_done, 1)
                    else:
                        mm.then_inc(y_ready, 1)

            project(0, BANKS)
            turn(0, BANKS)

            def chunk(c, par):
                for i in range(IC):
                    for a in range(PL - 1):
                        gate_up(c, par, i * PL + a)
                    if i == 2 and not last(c):
                        project(c + 1, FIRST_BANKS)
                    if i == 3 and not last(c):
                        turn(c + 1, FIRST_BANKS)
                    if i > 0:
                        down(c, i - 1)
                    elif not (isinstance(c, int) and c == 0):
                        down(c - 1, IC - 1)
                    if i == 2 and not last(c):
                        project(c + 1, LAST_BANKS)
                    if i == 3 and not last(c):
                        turn(c + 1, LAST_BANKS)
                    gate_up(c, par, i * PL + PL - 1)

            chunks(pe, chunk)
            down(NCH - 1, IC - 1)

        @block.scalar
        def _(act):
            def high(n):
                kind, i, h = STAGES[n]
                if kind == "down":
                    act.wait_ge(down_gated, 2 * i + h + 1)
                    at = i * PL + h * HALF
                    act.activation(w_down[:, 0, at:at + HALF, :], staged[n % 2][:, :, :], ACT.Copy).then_inc(w_high, 1)
                    return
                act.wait_ge(staged_loaded[n % 2], (n // 2 + 1) * 16)
                act.wait_ge(scale_step, SCALE_STEPS)
                w, which = (w_gate, 0) if kind == "gate" else (w_up, 1)
                for k in range(HALF):
                    op = act.activation(w[:, 0, h * HALF + k, i, :, :], staged[n % 2][:, k, :].rearrange("p (c a) -> p a c", a=PL),
                                        ACT.Identity, bias=0.0, scale=scale[:, which:which + 1])
                op.then_inc(w_high, 1)

            def deviation(c):
                wait(act, stat_step, c * (2 * BPC) + 2 * BPC)
                act.activation(std[:, :], mv[:, :, 1], ACT.Sqrt, bias=eps[:, :]).then_inc(std_ready, 1)

            def absolute(c, i, a):
                s = c * IC + i
                wait(act, hid_ready, s * PL + (a + 1))
                if a == 0:
                    wait(act, late_ready, s)
                act.activation(size[:, a, :], hid[i % 2][:, a, :], ACT.Abs).then_inc(size_ready, 1)

            def kept_parts(c, i):
                s = c * IC + i
                for a in range(PL):
                    wait(act, select_ready, s * PL + (a + 1))
                    if a == 0:
                        if i > 0:
                            wait(act, down_done, c * (IC - 1) + i)
                        else:
                            wait(act, y_ready, c * BPC)
                    act.activation(kept[:, 0, a, :], hid[i % 2][:, a, :], ACT.Copy).then_inc(kept_high, 1)

            SCALE_STEPS = 13
            for n in range(len(FIRST_STAGES)):
                if n == BEFORE:
                    deviation(0)
                high(n)

            def chunk(c, par):
                for i in range(IC):
                    for a in range(PL):
                        n = i * PL + a
                        wait(act, pair_ready, c * PPC + (n + 1))
                        wait(act, hid_ready, c * PPC + (n - 1))
                        act.activation(silu[n % 2][:, :], ring[2 * (n % 2)][:, :], ACT.Silu,
                                       scale=unscale[:, 0:1]).then_inc(silu_ready, 1)
                        absolute(c, i, a)
                        if a == 0 and i > 0:
                            kept_parts(c, i - 1)
                        elif a == 0 and not (isinstance(c, int) and c == 0):
                            kept_parts(c - 1, IC - 1)
                        if isinstance(c, int) and c == 0:
                            for n in staged_with(i, a):
                                high(n)
                        if a == PL - 2 and i == 2 and not last(c):
                            deviation(c + 1)

            chunks(act, chunk)
            kept_parts(NCH - 1, IC - 1)

        @block.vector
        def _(dve):
            steps = [0]

            def chained(op):
                steps[0] += 1
                op.then_inc(scale_step, 1)
                dve.wait_ge(scale_step, steps[0])

            ROOT_E = float(E) ** 0.5
            chained(dve.tensor_copy(bound[:, 0:2], sizes[:, 0:2]))
            chained(dve.tensor_tensor(bound[:, 2:3], sizes[:, 2:3], sizes[:, 5:6], ALU.mult))
            chained(dve.tensor_tensor(bound[:, 3:4], sizes[:, 3:4], sizes[:, 4:5], ALU.add))
            chained(dve.tensor_scalar(bound[:, 3:4], bound[:, 3:4], ROOT_E * 1.01, None, ALU.mult))
            chained(dve.tensor_scalar(bound[:, :], bound[:, :], TINY, None, ALU.max))
            chained(dve.tensor_scalar(power[:, :].bitcast(I32), bound[:, :].bitcast(I32), EXPONENT, None, ALU.bitwise_and))
            chained(dve.reciprocal(inverse[:, :], power[:, :]))
            chained(dve.tensor_scalar(scale[:, 0:4], inverse[:, 0:4], 2.0 ** 13, None, ALU.mult))
            chained(dve.tensor_scalar(root[:, :], inverse[:, 0:2], inverse[:, 3:4], 2.0, ALU.mult, ALU.mult))
            chained(dve.tensor_tensor(kept_scale[:, :], root[:, 0:1], root[:, 1:2], ALU.mult))
            chained(dve.reciprocal(unscale[:, 2:3], kept_scale[:, :]))
            chained(dve.tensor_scalar(unscale[:, 0:2], power[:, 0:2], power[:, 3:4], 2.0 ** -26, ALU.mult, ALU.mult))
            chained(dve.tensor_scalar(unscale[:, 2:3], unscale[:, 2:3], power[:, 2:3], 2.0 ** -13, ALU.mult, ALU.mult))
            dve.tensor_scalar(unscale[:, 1:2], unscale[:, 1:2], kept_scale[:, :], None, ALU.mult).then_inc(scale_step, 1)
            dve.tensor_scalar(shift_b[:, :], cols[:, 2, :], scale[:, 3:4], None, ALU.mult).then_inc(scale_step, 1)
            dve.tensor_scalar(scale_b[:, :], cols[:, 3, :], scale[:, 3:4], None, ALU.mult).then_inc(scale_step, 1)
            steps[0] += 3

            def rest(n):
                kind, i, h = STAGES[n]
                dve.wait_ge(staged_loaded[n % 2], (n // 2 + 1) * 16)
                if kind == "down":
                    for a in range(HALF):
                        op = dve.scalar_tensor_tensor(out=staged[n % 2][:, a, :], in0=staged[n % 2][:, a, :], scalar=scale[:, 2:3],
                                                      in1=keep["gate_b"][:, :], op0=ALU.mult, op1=ALU.mult)
                    op.then_inc(down_gated, 1)
                    at = i * PL + h * HALF
                    dve.wait_ge(w_high, n + 1)
                    dve.tensor_tensor(w_down[:, 1, at:at + HALF, :], staged[n % 2][:, :, :],
                                      w_down[:, 0, at:at + HALF, :], ALU.subtract).then_inc(w_rest, 1)
                    return
                w, which = (w_gate, 0) if kind == "gate" else (w_up, 1)
                dve.wait_ge(w_high, n + 1)
                for k in range(HALF):
                    row = h * HALF + k
                    op = dve.scalar_tensor_tensor(out=w[:, 1, row, i, :, :], in0=staged[n % 2][:, k, :].rearrange("p (c a) -> p a c", a=PL),
                                                  scalar=scale[:, which:which + 1], in1=w[:, 0, row, i, :, :],
                                                  op0=ALU.mult, op1=ALU.subtract)
                op.then_inc(w_rest, 1)

            def norm(c, par):
                wait(dve, x_loaded[par], dmas(c, par) + 16)
                for n, b in enumerate(BANKS):
                    wait(dve, projected, c * BPC + (n + 1))
                    dve.tensor_tensor(x_mid[par][:, b, :], ring[b][:, :], x_mid[par][:, b, :], ALU.add).then_inc(mid_ready, 1)
                    wait(dve, mid_ready, c * BPC + (n + 1))
                    dve.bn_stats(stats[:, b, :], x_mid[par][:, b, :]).then_inc(stat_step, 1)
                wait(dve, stat_step, c * (2 * BPC) + BPC)
                dve.sem_inc(norm_open, 1)
                for b in range(BPC):
                    dve.bn_aggr(mv[:, b, :], stats[:, b, :]).then_inc(stat_step, 1)
                wait(dve, std_ready, c + 1)
                dve.reciprocal(rstd[:, :], std[:, :]).then_inc(rstd_ready, 1)
                wait(dve, rstd_ready, c + 1)
                for b in range(BPC):
                    dve.tensor_scalar(xn[:, b, :], x_mid[par][:, b, :], mv[:, b, 0:1], rstd[:, b:b + 1],
                                      ALU.subtract, ALU.mult).then_inc(xn_ready, 1)

            def modulate(c, par):
                for n, k in enumerate(BANKS):
                    wait(dve, xT_ready, c * KT + (n + 1))
                    wait(dve, hT_ready, c * KT + n)
                    dve.tensor_scalar(turned[:, :], ring[k][:, :], scale_b[:, k:k + 1], shift_b[:, k:k + 1],
                                      ALU.mult, ALU.add).then_inc(turned_ready, 1)
                    wait(dve, turned_ready, c * KT + (n + 1))
                    dve.tensor_copy(hT[par][:, 0, k, :], turned[:, :]).then_inc(high_ready, 1)
                    wait(dve, high_ready, c * KT + (n + 1))
                    dve.tensor_tensor(hT[par][:, 1, k, :], turned[:, :], hT[par][:, 0, k, :], ALU.subtract).then_inc(hT_ready, 1)

            def hidden(c, i, a):
                s, n = c * IC + i, i * PL + a
                if a == 0:
                    wait(dve, kept_ready, s - 1)
                    wait(dve, size_ready, (s - 1) * PL)
                wait(dve, silu_ready, s * PL + (a + 1))
                dve.scalar_tensor_tensor(out=hid[i % 2][:, a, :], in0=ring[2 * (n % 2) + 1][:, :], scalar=unscale[:, 1:2],
                                         in1=silu[n % 2][:, :], op0=ALU.mult, op1=ALU.mult).then_inc(hid_ready, 1)


            def compare_early(c, i):
                s = c * IC + i
                wait(dve, size_ready, s * PL + 3)
                wait(dve, select_ready, s * PL)
                dve.tensor_tensor(early[:, 0, :], size[:, 0, :], size[:, 1, :], ALU.is_ge).then_inc(early_ready, 1)
                dve.tensor_tensor(early[:, 1:3, :], size[:, 0:2, :], size[:, 2:3, :].broadcast_to([P, 2, CHUNK]), ALU.is_ge).then_inc(early_ready, 1)
                wait(dve, early_ready, s * 2 + 2)
                dve.tensor_tensor(score[:, 0, :], early[:, 0, :], early[:, 1, :], ALU.add).then_inc(part_ready, 1)
                dve.tensor_tensor(score[:, 1, :], early[:, 2, :], early[:, 0, :], ALU.subtract).then_inc(part_ready, 1)
                dve.tensor_tensor(score[:, 2, :], early[:, 1, :], early[:, 2, :], ALU.add).then_inc(part_ready, 1)

            def compare_late(c, i):
                s = c * IC + i
                wait(dve, size_ready, s * PL + PL)
                dve.tensor_tensor(late[:, :, :], size[:, 0:3, :], size[:, 3:4, :].broadcast_to([P, 3, CHUNK]), ALU.is_ge).then_inc(late_ready, 1)
                wait(dve, late_ready, s + 1)
                wait(dve, part_ready, s * 4 + 3)
                dve.tensor_tensor(score[:, 3, :], late[:, 0, :], late[:, 1, :], ALU.add).then_inc(part_ready, 1)
                dve.tensor_tensor(score[:, 0:2, :], score[:, 0:2, :], late[:, 0:2, :], ALU.add).then_inc(score_ready, 1)
                dve.tensor_tensor(score[:, 2, :], late[:, 2, :], score[:, 2, :], ALU.subtract).then_inc(score_ready, 1)
                wait(dve, part_ready, s * 4 + 4)
                dve.tensor_tensor(score[:, 3, :], score[:, 3, :], late[:, 2, :], ALU.add).then_inc(score_ready, 1)

            def select(c, i):
                s = c * IC + i
                here = hid[i % 2]
                wait(dve, score_ready, s * 3 + 3)
                for a, (test, least) in enumerate(((ALU.is_ge, 2.0), (ALU.is_ge, 1.0), (ALU.is_ge, 0.0), (ALU.is_le, 1.0))):
                    dve.scalar_tensor_tensor(out=here[:, a, :], in0=score[:, a, :], scalar=least,
                                             in1=here[:, a, :], op0=test, op1=ALU.mult).then_inc(select_ready, 1)
                for b in range(2):
                    wait(dve, kept_high, s * PL + 2 * (b + 1))
                    op = dve.tensor_tensor(kept[:, 1, 2 * b:2 * b + 2, :], here[:, 2 * b:2 * b + 2, :],
                                           kept[:, 0, 2 * b:2 * b + 2, :], ALU.subtract)
                op.then_inc(kept_ready, 1)

            def add(c, par):
                for b in range(BPC):
                    wait(dve, y_ready, c * BPC + (b + 1))
                    dve.scalar_tensor_tensor(out=x_mid[par][:, b, :], in0=y_ps[b][:, :], scalar=unscale[:, 2:3],
                                             in1=x_mid[par][:, b, :], op0=ALU.mult, op1=ALU.add).then_inc(out_ready, 1)

            def split_weights(c, i, a):
                if isinstance(c, int) and c == 0:
                    for n in staged_with(i, a):
                        rest(n)

            for n in range(BEFORE):
                rest(n)
            norm(0, 0)
            dve.wait_ge(scale_step, steps[0])
            for n in range(BEFORE, len(FIRST_STAGES)):
                rest(n)
            modulate(0, 0)

            def chunk(c, par):
                for i in range(IC):
                    hidden(c, i, 0)
                    if i > 0:
                        select(c, i - 1)
                    elif not (isinstance(c, int) and c == 0):
                        select(c - 1, IC - 1)
                    split_weights(c, i, 0)
                    hidden(c, i, 1)
                    split_weights(c, i, 1)
                    hidden(c, i, 2)
                    compare_early(c, i)
                    split_weights(c, i, 2)
                    if i == 0 and not (isinstance(c, int) and c == 0):
                        add(c - 1, 1 - par)
                    if i == 2 and not last(c):
                        norm(c + 1, 1 - par)
                    if i == 3 and not last(c):
                        modulate(c + 1, 1 - par)
                    hidden(c, i, 3)
                    compare_late(c, i)

            chunks(dve, chunk)
            select(NCH - 1, IC - 1)
            add(NCH - 1, (NCH - 1) % 2)


def adaln_kernel(nc, ins, out):
    qk_scr = nc.dram_tensor("qk_scr", [2, 2 * E, N], F32).ap()
    v_scr = nc.dram_tensor("v_scr", [N, E], F32).ap()
    att_scr = nc.dram_tensor("att_scr", [E, N], F32).ap()
    with ExitStack() as ctx:
        sb = lambda name, shape: ctx.enter_context(nc.sbuf_tensor(name, shape, F32))
        keep = {
            "ident": sb("ident", [P, P]),
            "gate_a": sb("gate_a", [P, E]),
            "gate_b": sb("gate_b", [P, E]),
            "cols": sb("cols", [P, 4, KT]),
            "qk_scale": sb("qk_scale", [P, 1]),
            "qk_bias": sb("qk_bias", [P, 1]),
            "eps": sb("eps", [P, 1]),
            "sizes": sb("sizes", [P, 6]),
            "w_out": sb("w_out", [P, KT * E]),
            "feed": sb("feed", [P, NG * CHUNK]),
        }
        with ExitStack() as stacks:
            first_k = stacks.enter_context(nc.sbuf_tensor("first_k", [P, HPG, CHUNK], F32R))
            first_q = stacks.enter_context(nc.sbuf_tensor("first_q", [P, HPG, CHUNK], F32R))
            with ExitStack() as parts:
                w_parts = [parts.enter_context(nc.sbuf_tensor(f"wqkv_{part}", [P, KT, 3 * E], F32R)) for part in ("round", "rest")]
                setup_phase(nc, keep, w_parts, ins)
                projection_phase(nc, keep, w_parts, first_k, first_q, ins, qk_scr, v_scr)
            attention_phase(nc, keep, first_k, first_q, ins, qk_scr, v_scr, att_scr)
        mlp_phase(nc, keep, ins, att_scr, out)


_INS = {
    "x": "L0_attn_x", "w_qkv": "L0_attn_w_qkv", "w_out": "L0_attn_w_out", "ln_scale": "L0_attn_ln_scale",
    "ln_bias": "L0_attn_ln_bias", "w_gate": "L0_ffn_w_gate", "w_up": "L0_ffn_w_up", "w_down": "L0_ffn_w_down",
    "c": "L0_c", "wmod": "L0_wmod",
}


def rope_table():
    inv_freq = np.float32(1.0) / np.power(np.float32(ROPE_BASE), np.arange(0, D, 2, dtype=np.float32) / np.float32(D))
    angle = (np.arange(N, dtype=np.float32)[:, None] * inv_freq[None, :]).astype(np.float64)
    cos, sin = np.cos(angle), np.sin(angle)
    table = np.stack([np.concatenate([cos, cos], 1), np.concatenate([-sin, sin], 1)], 1)
    return table.astype(np.float32)


def kernel(**inputs):
    import concourse.bacc as _bacc
    from concourse.bass_utils import run_bass_kernel_spmd as _run

    nc = _bacc.Bacc("TRN2", target_bir_lowering=False, num_devices=1)
    arrays = {f"in_{short}": np.ascontiguousarray(inputs[name]) for short, name in _INS.items()}
    arrays["in_rope"] = rope_table()
    ins = {name[3:]: nc.dram_tensor(name, a.shape, mybir.dt.from_np(a.dtype), kind="ExternalInput").ap()
           for name, a in arrays.items()}
    out = nc.dram_tensor("out", (1, N, E), F32, kind="ExternalOutput").ap()
    adaln_kernel(nc, ins, out)
    r = _run(nc, [arrays], core_ids=[0])
    return r.results[0]["out"]
```
